# Optimizing a Trainium2 kernel written in Bass

```python
import numpy as np
import jax
import jax.numpy as jnp

def _softmax(x, axis=-1):
    return jax.nn.softmax(x, axis=axis)
def _gelu(x):
    return jax.nn.gelu(x, approximate=True)
def _silu(x):
    return jax.nn.silu(x)
def _sigmoid(x):
    return jax.nn.sigmoid(x)
def _layernorm(x, axis=-1, eps=1e-5):
    m = jnp.mean(x, axis=axis, keepdims=True)
    v = jnp.var(x, axis=axis, keepdims=True)
    return (x - m) / jnp.sqrt(v + eps)
def _scatter_add(tgt, idx, src, axis=0):
    return tgt.at[idx].add(src)
def _segment_sum(src, seg, n):
    return jax.ops.segment_sum(src, seg, n)

kernel_name = 'mk_conv_seq_d1_conv_nchw256_6c61c6'

def setup_inputs(seed: int = 0):
    np.random.seed(seed)
    _w = jnp.asarray
    def _rec_inputs():
        import jax
        import jax.numpy as jnp
        _gk = jax.random.key(seed)
        x = -0.0003482 + 1 * jax.random.normal(jax.random.fold_in(_gk, 1), (8, 256, 96, 96), jnp.float32)
        return x
    x = _rec_inputs()
    def _L0_conv_setup():
        import jax, jax.numpy as jnp
        import numpy as np
        B, C, H, W = (8, 256, 96, 96)
        HEADS, WS = (8, 12)
        HD = C // HEADS
        SCALE = HD ** (-0.5)
        L = WS * WS

        def _rel_index(ws):
            coords = np.stack(np.meshgrid(np.arange(ws), np.arange(ws), indexing='ij')).reshape(2, -1)
            rel = (coords[:, :, None] - coords[:, None, :]).transpose(1, 2, 0) + (ws - 1)
            return rel[..., 0] * (2 * ws - 1) + rel[..., 1]
        REL_IDX = jnp.asarray(_rel_index(WS).reshape(-1))

        def dct1(x):
            n = x.shape[-1]
            xv = jnp.concatenate([x, x[..., ::-1]], axis=-1)
            X = jnp.fft.rfft(xv, axis=-1)[..., :n]
            k = jnp.arange(n, dtype=jnp.float32)
            Wc = jnp.exp(-1j * jnp.pi * k / (2 * n))
            return (X * Wc).real.astype(jnp.float32)

        def dct2(x):
            x = dct1(x.swapaxes(-1, -2)).swapaxes(-1, -2)
            return dct1(x)

        def idct1(X):
            n = X.shape[-1]
            k = jnp.arange(n, dtype=jnp.float32)
            Wc = jnp.exp(1j * jnp.pi * k / (2 * n))
            Xc = X.astype(jnp.complex64) * Wc
            Xc_full = jnp.concatenate([Xc, Xc[..., 1:-1][..., ::-1]], axis=-1)
            x = jnp.fft.irfft(Xc_full, n=2 * n, axis=-1)
            return x[..., :n].astype(jnp.float32)

        def idct2(x):
            x = idct1(x.swapaxes(-1, -2)).swapaxes(-1, -2)
            return idct1(x)

        def conv2d(x, w, groups=1, pad=0):
            return jax.lax.conv_general_dilated(x, w, (1, 1), [(pad, pad), (pad, pad)], dimension_numbers=('NCHW', 'OIHW', 'NCHW'), feature_group_count=groups)

        def batchnorm(x, g, b):
            m = x.mean(axis=(0, 2, 3), keepdims=True)
            v = x.var(axis=(0, 2, 3), keepdims=True)
            return (x - m) * jax.lax.rsqrt(v + 1e-05) * g.reshape(1, -1, 1, 1) + b.reshape(1, -1, 1, 1)
        key = jax.random.key(seed)
        ks = jax.random.split(key, 10)

        def rn(k, shape, s=0.02):
            return jax.random.normal(k, shape, dtype=jnp.float32) * s
        return {'x': jax.random.normal(ks[0], (B, C, H, W), dtype=jnp.float32), 'qkv_w': rn(ks[1], (3 * C, C)), 'qkv_b': jnp.zeros((3 * C,), jnp.float32), 'proj_w': rn(ks[2], (C, C)), 'proj_b': jnp.zeros((C,), jnp.float32), 'lpe_w': rn(ks[3], (C, 1, 3, 3), 0.1), 'lpe_b': jnp.zeros((C,), jnp.float32), 'lpe_scale': jnp.ones((1,), jnp.float32), 'rpb_table': rn(ks[4], ((2 * WS - 1) ** 2, HEADS), 0.02), 'ec_w': rn(ks[5], (1, 1, 3, 3), 0.3), 'bn1_g': jnp.ones((1,), jnp.float32), 'bn1_b': jnp.zeros((1,), jnp.float32), 'nl_w': rn(ks[6], (1, 1), 1.0), 'nl_b': jnp.zeros((1,), jnp.float32), 'fr_w': rn(ks[7], (C, C, 1, 1), 0.05), 'bn2_g': jnp.ones((C,), jnp.float32), 'bn2_b': jnp.zeros((C,), jnp.float32)}
    _L0_conv_all = _L0_conv_setup()
    _L0_conv_in = {k: v for k, v in _L0_conv_all.items() if k in ('qkv_w', 'qkv_b', 'proj_w', 'proj_b', 'lpe_w', 'lpe_b', 'lpe_scale', 'rpb_table', 'ec_w', 'bn1_g', 'bn1_b', 'nl_w', 'nl_b', 'fr_w', 'bn2_g', 'bn2_b', )}
    del _L0_conv_all

    return {
        "x": x,
        "L0_conv_qkv_w": _L0_conv_in["qkv_w"],
        "L0_conv_qkv_b": _L0_conv_in["qkv_b"],
        "L0_conv_proj_w": _L0_conv_in["proj_w"],
        "L0_conv_proj_b": _L0_conv_in["proj_b"],
        "L0_conv_lpe_w": _L0_conv_in["lpe_w"],
        "L0_conv_lpe_b": _L0_conv_in["lpe_b"],
        "L0_conv_lpe_scale": _L0_conv_in["lpe_scale"],
        "L0_conv_rpb_table": _L0_conv_in["rpb_table"],
        "L0_conv_ec_w": _L0_conv_in["ec_w"],
        "L0_conv_bn1_g": _L0_conv_in["bn1_g"],
        "L0_conv_bn1_b": _L0_conv_in["bn1_b"],
        "L0_conv_nl_w": _L0_conv_in["nl_w"],
        "L0_conv_nl_b": _L0_conv_in["nl_b"],
        "L0_conv_fr_w": _L0_conv_in["fr_w"],
        "L0_conv_bn2_g": _L0_conv_in["bn2_g"],
        "L0_conv_bn2_b": _L0_conv_in["bn2_b"],
    }

def reference(x, L0_conv_qkv_w, L0_conv_qkv_b, L0_conv_proj_w, L0_conv_proj_b, L0_conv_lpe_w, L0_conv_lpe_b, L0_conv_lpe_scale, L0_conv_rpb_table, L0_conv_ec_w, L0_conv_bn1_g, L0_conv_bn1_b, L0_conv_nl_w, L0_conv_nl_b, L0_conv_fr_w, L0_conv_bn2_g, L0_conv_bn2_b):
    import jax
    import jax.numpy as jnp
    def _L0_conv_ref(x, qkv_w, qkv_b, proj_w, proj_b, lpe_w, lpe_b, lpe_scale, rpb_table, ec_w, bn1_g, bn1_b, nl_w, nl_b, fr_w, bn2_g, bn2_b):
        import jax, jax.numpy as jnp
        import numpy as np
        B, C, H, W = (8, 256, 96, 96)
        HEADS, WS = (8, 12)
        HD = C // HEADS
        SCALE = HD ** (-0.5)
        L = WS * WS

        def _rel_index(ws):
            coords = np.stack(np.meshgrid(np.arange(ws), np.arange(ws), indexing='ij')).reshape(2, -1)
            rel = (coords[:, :, None] - coords[:, None, :]).transpose(1, 2, 0) + (ws - 1)
            return rel[..., 0] * (2 * ws - 1) + rel[..., 1]
        REL_IDX = jnp.asarray(_rel_index(WS).reshape(-1))

        def dct1(x):
            n = x.shape[-1]
            xv = jnp.concatenate([x, x[..., ::-1]], axis=-1)
            X = jnp.fft.rfft(xv, axis=-1)[..., :n]
            k = jnp.arange(n, dtype=jnp.float32)
            Wc = jnp.exp(-1j * jnp.pi * k / (2 * n))
            return (X * Wc).real.astype(jnp.float32)

        def dct2(x):
            x = dct1(x.swapaxes(-1, -2)).swapaxes(-1, -2)
            return dct1(x)

        def idct1(X):
            n = X.shape[-1]
            k = jnp.arange(n, dtype=jnp.float32)
            Wc = jnp.exp(1j * jnp.pi * k / (2 * n))
            Xc = X.astype(jnp.complex64) * Wc
            Xc_full = jnp.concatenate([Xc, Xc[..., 1:-1][..., ::-1]], axis=-1)
            x = jnp.fft.irfft(Xc_full, n=2 * n, axis=-1)
            return x[..., :n].astype(jnp.float32)

        def idct2(x):
            x = idct1(x.swapaxes(-1, -2)).swapaxes(-1, -2)
            return idct1(x)

        def conv2d(x, w, groups=1, pad=0):
            return jax.lax.conv_general_dilated(x, w, (1, 1), [(pad, pad), (pad, pad)], dimension_numbers=('NCHW', 'OIHW', 'NCHW'), feature_group_count=groups)

        def batchnorm(x, g, b):
            m = x.mean(axis=(0, 2, 3), keepdims=True)
            v = x.var(axis=(0, 2, 3), keepdims=True)
            return (x - m) * jax.lax.rsqrt(v + 1e-05) * g.reshape(1, -1, 1, 1) + b.reshape(1, -1, 1, 1)
        freq = jnp.abs(dct2(x))
        mn = freq.min(axis=(2, 3), keepdims=True)
        mx = freq.max(axis=(2, 3), keepdims=True)
        freq_norm = (freq - mn) / (mx + 1e-06)
        local_energy = jax.nn.relu(batchnorm(conv2d(freq_norm.mean(axis=1, keepdims=True), ec_w, pad=1), bn1_g, bn1_b))
        pooled = local_energy.mean(axis=(2, 3))
        noise_global = jax.nn.sigmoid(pooled @ nl_w.T + nl_b)
        noise_mask = jax.nn.sigmoid(1.0 - local_energy) * noise_global.reshape(B, 1, 1, 1)
        xh = x.transpose(0, 2, 3, 1)
        win = xh.reshape(B, H // WS, WS, W // WS, WS, C).transpose(0, 1, 3, 2, 4, 5).reshape(-1, L, C)
        qkv = (win @ qkv_w.T + qkv_b).reshape(-1, L, 3, HEADS, HD).transpose(2, 0, 3, 1, 4)
        q, k, v = (qkv[0], qkv[1], qkv[2])
        attn = jnp.einsum('bhld,bhmd->bhlm', q, k) * SCALE
        bias = rpb_table[REL_IDX].reshape(L, L, HEADS).transpose(2, 0, 1)
        attn = jax.nn.softmax(attn + bias[None], axis=-1)
        out = jnp.einsum('bhlm,bhmd->bhld', attn, v).transpose(0, 2, 1, 3).reshape(-1, L, C)
        out = out @ proj_w.T + proj_b
        x_attn = out.reshape(B, H // WS, W // WS, WS, WS, C).transpose(0, 1, 3, 2, 4, 5).reshape(B, H, W, C)
        x_lpe = (conv2d(x, lpe_w, groups=C, pad=1) + lpe_b.reshape(1, C, 1, 1)) * lpe_scale * noise_mask
        x_attn_img = x_attn.transpose(0, 3, 1, 2) + x_lpe
        freq2 = dct2(x_attn_img)
        freq_mean = freq2.mean(axis=(2, 3), keepdims=True)
        gate = jax.nn.sigmoid(5.0 * (jnp.abs(freq2) - freq_mean))
        x_freq = idct2(freq2 * gate)
        y = batchnorm(conv2d(x + x_freq, fr_w), bn2_g, bn2_b)
        return jax.nn.gelu(y, approximate=False)

    def _gn(v, G=32, eps=1e-5):
        B_, C_, H_, W_ = v.shape
        g = v.reshape(B_, G, C_ // G, H_, W_)
        m = jnp.mean(g, axis=(2, 3, 4), keepdims=True)
        s = jnp.var(g, axis=(2, 3, 4), keepdims=True)
        return ((g - m) / jnp.sqrt(s + eps)).reshape(v.shape)

    def _ln_c(v, eps=1e-6):
        m = jnp.mean(v, axis=1, keepdims=True)
        s = jnp.var(v, axis=1, keepdims=True)
        return (v - m) / jnp.sqrt(s + eps)

    def _ln_t(v, eps=1e-5):
        m = jnp.mean(v, axis=-1, keepdims=True)
        s = jnp.var(v, axis=-1, keepdims=True)
        return (v - m) / jnp.sqrt(s + eps)

    def _to_tokens(v):
        B_, C_, H_, W_ = v.shape
        return v.reshape(B_, C_, H_ * W_).transpose(0, 2, 1)
    def _from_tokens(t, like):
        B_, C_, H_, W_ = like.shape
        return t.transpose(0, 2, 1).reshape(B_, C_, H_, W_)

    x = _L0_conv_ref(x, L0_conv_qkv_w, L0_conv_qkv_b, L0_conv_proj_w, L0_conv_proj_b, L0_conv_lpe_w, L0_conv_lpe_b, L0_conv_lpe_scale, L0_conv_rpb_table, L0_conv_ec_w, L0_conv_bn1_g, L0_conv_bn1_b, L0_conv_nl_w, L0_conv_nl_b, L0_conv_fr_w, L0_conv_bn2_g, L0_conv_bn2_b)
    return x


_drawn_inputs = setup_inputs


def setup_inputs(seed=0):
    import zlib

    import numpy as np

    out = dict(_drawn_inputs(seed))
    spreads = {'L0_conv_qkv_b': (0.0, 0.8),
     'L0_conv_proj_b': (0.0, 2.0),
     'L0_conv_lpe_b': (0.0, 2.0),
     'L0_conv_bn2_g': (1.0, 0.2),
     'L0_conv_bn2_b': (0.0, 0.1)}
    factors = {'L0_conv_qkv_w': 6.525,
     'L0_conv_proj_w': 6.416,
     'L0_conv_rpb_table': 8.0,
     'L0_conv_ec_w': 27.079}
    for name, (base, spread) in spreads.items():
        noise = np.random.default_rng([zlib.crc32(name.encode()), seed]).standard_normal(out[name].shape)
        drawn = base * np.exp(spread * noise) if base else spread * noise
        out[name] = jnp.asarray(drawn.astype(out[name].dtype))
    for name, factor in factors.items():
        out[name] = (out[name] * factor).astype(out[name].dtype)
    return out
```

```python
import math
from contextlib import ExitStack

import numpy as np
import concourse.bass as bass
from concourse import mybir
from concourse.alu_op_type import AluOpType as ALU

ACT = mybir.ActivationFunctionType
AX = mybir.AxisListType
F32 = mybir.dt.float32
U32 = mybir.dt.uint32

C, H, W = 256, 96, 96
HEADS, WS, HD = 8, 12, 32
L = WS * WS
HL = L // 2
CT = C // 128
HG = 4
LC = 5
QN = 2 * L + 16
NS = H // WS
NP = W // (2 * WS)
NT = NP * 4
SW = WS * W
SCALE = HD ** -0.5
NCH = C // 4
NG = H // 4
HW = H * W
BIG = 3.0e38


def shape_constants():
    k = np.arange(96)
    cos = np.cos(np.pi * np.outer(2 * k + 1, k) / 192)
    dct = 2 * cos
    inv = np.where(k[:, None] == 0, 1.0, 2.0) * cos.T / 192
    inv[94] += math.cos(math.pi * 94 / 192) * (-1.0) ** k / 192
    rowsum = dct.sum(1)
    shifts = np.zeros((96, 3, 96))
    for d in range(3):
        for y in range(96):
            if 0 <= y + d - 1 < 96:
                shifts[y + d - 1, d, y] = 1
    blocks = np.zeros((128, HG, 32))
    for j in range(HG):
        blocks[32 * j:32 * j + 32, j] = 1
    f = lambda a: np.ascontiguousarray(a, np.float32)
    return {
        "c_dct": f(np.concatenate([dct, rowsum[:, None]], 1)),
        "c_mean": f(np.repeat(rowsum[:, None] / (96 * 96), 96, 1)),
        "c_inv": f(inv),
        "c_shift": f(shifts.reshape(96, 288)),
        "c_block": f(blocks.reshape(128, 128)),
        "c_eye": f(np.eye(128)),
    }


def build(nc, a, out, B):
    NSTRIP = B * NS
    yscr = nc.dram_tensor("y_scratch", [B, C, HW], F32, kind="Internal").ap()
    bscr = nc.dram_tensor("bias_scratch", [L, HEADS, L], F32, kind="Internal").ap()
    x = a["x"]

    with ExitStack() as ctx:
        def sb(name, shape):
            return ctx.enter_context(nc.sbuf_tensor(name, shape, F32))

        def sem(name):
            return ctx.enter_context(nc.semaphore(name))

        wqkv = sb("wqkv", [128, CT, 3 * C])
        wproj = sb("wproj", [128, CT, C])
        wfr = sb("wfr", [128, CT, C])
        negbias = sb("negbias", [128, CT, LC, L])
        dct = sb("dct", [96, 97])
        meanm = sb("meanm", [96, 96])
        inv = sb("inv", [96, 96])
        block1 = sb("block1", [128, HG, 32])
        eye = sb("eye", [128, 128])
        qb = sb("qb", [128, 6])
        nqb = sb("nqb", [128, CT])
        pb = sb("pb", [96, C])
        lw = sb("lw", [128, CT, 9])
        lb = sb("lb", [128, CT])
        mask = sb("mask", [96, B, 96])
        agg = sb("agg", [128, CT, B, 3])
        bn2 = sb("bn2", [128, 2, CT])
        bn2s = sb("bn2s", [128, 6, CT])
        zrow = sb("zrow", [128, CT, W])
        tick = sb("tick", [128, 4])
        AH = sb("AH", [128, C * 96])
        xs = sb("xs", [128, CT, WS + 2, W])
        WORKN = 17568
        work = sb("work", [128, WORKN])
        used = {}

        def carve(phase, *shape):
            n = int(np.prod(shape))
            at = used.get(phase, 0)
            used[phase] = at + n
            assert at + n <= WORKN, (phase, at + n)
            v = work[:, at:at + n]
            names = "abcd"[:len(shape)]
            return v if len(shape) == 1 else v.rearrange(
                f"p ({' '.join(names)}) -> p {' '.join(names)}", **dict(zip(names[1:], shape[1:])))

        A = AH[0:96, :].rearrange("p (c h) -> p c h", h=96)
        xw = [carve("a", CT, QN) for _ in range(2)]
        q_sb = [carve("a", CT, QN) for _ in range(2)]
        k_sb = [carve("a", CT, 2 * L) for _ in range(2)]
        v_sb = [carve("a", 2, 2, C) for _ in range(2)]
        qbd = [carve("a", LC, HG, 32) for _ in range(2)]
        sp = [carve("a", LC, L) for _ in range(4)]
        pt = [carve("a", LC, 2, 128) for _ in range(2)]
        ostrip = carve("a", CT, WS, W)
        lpe = carve("a", CT, WS, W)
        mn = [carve("a", LC) for _ in range(4)]
        den = [carve("a", LC) for _ in range(4)]
        rden = [carve("a", LC) for _ in range(4)]
        mrow = carve("a", WS)
        rowt = [carve("a", C) for _ in range(2)]
        b1 = [carve("f", 4, 97) for _ in range(2)]
        tg = [carve("f", 4, 96) for _ in range(2)]
        gs = [carve("f", 4, 96) for _ in range(2)]
        msb = [carve("f", 4) for _ in range(2)]
        xc = [carve("f", CT, 384) for _ in range(2)]
        zs = [carve("f", CT, 384) for _ in range(2)]
        ys = [carve("f", CT, 384) for _ in range(2)]
        stats = carve("f", CT, NG, 6)
        ag = carve("f", CT, 2)
        xg = [carve("n", 16, 96) for _ in range(8)]
        mm = carve("n", 2, 24)
        mx = carve("n", 4)
        emap = AH[0:96, 96 * 256 - 98 * B:].rearrange("p (b k) -> p b k", b=B)
        erows = carve("n", 2304)
        emt = AH[0:96, 224 * 96:225 * 96]
        esum = AH[0:96, 225 * 96:(225 + B) * 96].rearrange("p (b l) -> p b l", b=B)
        rrep = carve("n", 32)
        shift = carve("n", 3, 96)
        taps = carve("n", 9)
        band = carve("n", 3, 96)
        cmap = carve("n", B, 96)
        le = carve("n", B, 96)
        sc = carve("n", 32)
        st6 = carve("n", B, 6)
        accb = carve("n", B)
        ngb = carve("n", B)
        ones = carve("n", 96)
        ones96 = carve("n", 96)
        NB1 = A[:, 0:128, :]
        NF = AH[:, 128 * 96:128 * 96 + 96 * 96].rearrange("p (k l) -> p k l", l=96)

        ps = ctx.enter_context(nc.psum_tensor("ps", [128, 8, 512], F32))
        psS = [ps[:, 0:2, :], ps[:, 2:4, :]]
        psT = [4, 5]
        psO, psM = 6, 7

        S = {n: sem(n) for n in (
            "consts_in taps_in setup_vec setup_pool bias_rows bias_in "
            "n_st1 n_b1 n_st2 n_f n_chain n_r n_e n_free n_erow n_emt n_et n_ec "
            "m_band m_conv m_cmap m_chain m_mean_in m_mean m_var_in m_var m_sqrt_in m_sqrt m_ab m_le m_pool "
            "m_ng m_sig m_done "
            "xs_in xw_ready piece piece_out qbd_ready scores sb_ready exp_done rden_ready norm_done "
            "ptrans pt_a pt_d av o_out lpe_step row_ps row_mask a_row mrow_ready strip_done "
            "f1 b1_ready f2 abs_ready tg_ready gate_ready g_ready i1 h_ready xc_in0 xc_in1 zps z_ready yps y_ready "
            "stat y_out0 y_out1 agg_step "
            "bnf_step bnf_sqrt_in bnf_sqrt bnf_ready").split()}
        n_x = [sem(f"n_x{i}") for i in range(8)]
        f_in = [sem(f"f_in{i}") for i in range(8)]
        f_gelu = [sem(f"f_gelu{i}") for i in range(8)]
        f_out = [sem(f"f_out{i}") for i in range(8)]
        fb = [AH[:, 2304 * i:2304 * (i + 1)] for i in range(8)]
        NCONST, NTAPS, NBIAS = 15, 6, 4 * LC

        def bc(v, n):
            return v.rearrange("(a n) -> a n", a=1).broadcast_to([n, v.shape[0]])

        def wait_apart(eng, *waits):
            values = [v if isinstance(v, int) else eng.snap(v) for _, v in waits]
            for value in values:
                eng.compute_val(value)
            eng.wait_ge(S["consts_in"], 16 * NCONST)
            for (which, _), value in zip(waits, values):
                eng.wait_ge(which, value)

        def pieces_at(t):
            p, k = (t + 1) // 4 + 1, (t + 1) % 4
            if t == 0:
                return list(range(6, 10))
            return [6 * p + 2 * k, 6 * p + 2 * k + 1] if p < NP and k < 3 else []

        def strips(eng):
            return eng.Fori(0, NS)

        block = ctx.enter_context(nc.Block())

        @block.sync
        def _(sy):
            for dst, src in (
                (wqkv[:], a["wqkvT"].rearrange("(t p) n -> p t n", p=128)),
                (wproj[:], a["wprojT"].rearrange("(t p) n -> p t n", p=128)),
                (wfr[:], a["wfrT"].rearrange("(t p) n -> p t n", p=128)),
                (dct[:], a["c_dct"]), (meanm[:], a["c_mean"]), (inv[:], a["c_inv"]),
                (block1[:].rearrange("p a b -> p (a b)"), a["c_block"]), (eye[:], a["c_eye"]),
                (qb[:], a["qkv_b"]),
                (pb[:], bc(a["proj_b"], 96)),
                (lw[:], a["lpe_w"].rearrange("(t p) n -> p t n", p=128)),
                (lb[:], a["lpe_b"]),
                (bn2[:, 0, :], a["bn2_g"]),
                (bn2[:, 1, :], a["bn2_b"]),
                (shift[0:96], a["c_shift"].rearrange("p (a b) -> p a b", a=3)),
            ):
                sy.dma_start(dst, src).then_inc(S["consts_in"], 16)
            for dst, src in ((taps[0:96], a["ec_w"]), (sc[0:96, 0:1], a["bn1_g"]), (sc[0:96, 1:2], a["bn1_b"]),
                             (sc[0:96, 2:3], a["nl_w"]), (sc[0:96, 3:4], a["nl_b"]), (sc[0:96, 4:5], a["lpe_scale"])):
                sy.dma_start(dst, bc(src, 96)).then_inc(S["taps_in"], 16)

            def load_units(b, first):
                for ct in range(CT):
                    u = b * CT + ct
                    for g in range(8):
                        if not first or ct:
                            sy.wait_ge(S["n_st1"], u * 32 + 4 * (g + 1) - 32)
                        sy.dma_start(xg[g][0:96],
                                     x[bass.ds(b, 1), ct * 128 + 16 * g:ct * 128 + 16 * g + 16]
                                     .rearrange("b c h w -> h (b c) w")).then_inc(n_x[g], 16)
            load_units(0, True)
            if B > 1:
                with sy.Fori(1, B) as b:
                    load_units(b, False)
            sy.wait_ge(S["m_done"], 1)

            def load_strip(b, s, where):
                xi = x[bass.ds(b, 1)].rearrange("b (t p) h w -> p (b t) h w", p=128)
                rows = [(0, s * WS - 1, 1), (1, s * WS, WS), (WS + 1, s * WS + WS, 1)]
                for at, r0, n in rows:
                    if (where == "top" and at == 0) or (where == "bottom" and at == WS + 1):
                        sy.dma_start(xs[:, :, at, :], zrow[:]).then_inc(S["xs_in"], 16)
                    else:
                        sy.dma_start(xs[:, :, at:at + n, :], xi[:, :, bass.ds(r0, n), :]).then_inc(S["xs_in"], 16)

            def after_strip(b, s):
                n = b * NS + s
                wait_apart(sy, (S["xw_ready"], n * NP), (S["lpe_step"], n * 18))

            with sy.Fori(0, B) as b:
                load_strip(b, 0, "top")
                with sy.Fori(1, NS - 1) as s:
                    after_strip(b, s)
                    load_strip(b, s, "inner")
                after_strip(b, NS - 1)
                load_strip(b, NS - 1, "bottom")
                wait_apart(sy, (S["strip_done"], (b + 1) * (NS * 4)))
                xi = x[bass.ds(b, 1)].rearrange("b (t p) h w -> p (b t) (h w)", p=128)
                yi = yscr[bass.ds(b, 1)].rearrange("b (t p) n -> p (b t) n", p=128)

                def load_x(g, par):
                    sy.dma_start(xc[par], xi[:, :, bass.ds(g * 384, 384)]).then_inc(S[f"xc_in{par}"], 16)

                def store_y(g, par):
                    wait_apart(sy, (S["y_ready"], b * NG + g + 1))
                    sy.dma_start(yi[:, :, bass.ds(g * 384, 384)], ys[par]).then_inc(S[f"y_out{par}"], 16)

                load_x(0, 0)
                load_x(1, 1)
                with sy.Fori(0, NG // 2 - 1) as i:
                    for par in range(2):
                        store_y(i * 2 + par, par)
                        load_x(i * 2 + 2 + par, par)
                for par in range(2):
                    store_y(NG - 2 + par, par)
                wait_apart(sy, *[(S[f"y_out{par}"], b * (NG * 8) + NG * 8) for par in range(2)],
                           (S["agg_step"], b * 7 + 7))

            def load_f(b, first):
                yi = yscr[bass.ds(b, 1)].rearrange("b (t p) n -> p (b t) n", p=128)
                for k in range(8):
                    if not first:
                        sy.wait_ge(f_out[k], b * 16)
                    sy.dma_start(fb[k], yi[:, k // 4, 2304 * (k % 4):2304 * (k % 4 + 1)]).then_inc(f_in[k], 16)
            load_f(0, True)
            if B > 1:
                with sy.Fori(1, B) as b:
                    load_f(b, False)

        @block.gpsimd
        def _(g):
            g.memset(negbias[:], 0.0).then_inc(S["setup_pool"], 1)
            g.memset(zrow[:], 0.0).then_inc(S["setup_pool"], 1)
            g.memset(emap, 0.0).then_inc(S["setup_pool"], 1)
            g.memset(ones, 1.0).then_inc(S["setup_pool"], 1)
            g.memset(ones96[0:96], 1.0 / 96).then_inc(S["setup_pool"], 1)
            g.memset(tick[:, 3:4], 0.0).then_inc(S["setup_pool"], 1)
            g.memset(tick[:, 0:1], 0.0).then_inc(S["n_free"], 1)
            g.wait_ge(S["setup_pool"], 6)
            tab = a["rpb_rev"]

            def sum_rows(u):
                wait_apart(g, (S["n_erow"], u + 1))
                for j in range(4):
                    g.dma_start(emt[24 * j:24 * j + 24, :], erows[32 * j:32 * j + 1, :]
                                .rearrange("p (k l) -> p k l", l=96)).then_inc(S["n_emt"], 16)

            def bias_rows(r):
                with g.Fori(0, WS) as c:
                    g.dma_start(bscr[bass.ds(r * WS + c, 1)].rearrange("a h (y x) -> (a h) y x", y=WS),
                                tab[:, bass.ds(r * -1 + (WS - 1), WS), bass.ds(c * -1 + (WS - 1), WS)]
                                ).then_inc(S["bias_rows"], 16)

            both = min(WS, B * CT)
            with g.Fori(0, both) as u:
                sum_rows(u)
                bias_rows(u)
            if both < WS:
                with g.Fori(both, WS) as r:
                    bias_rows(r)
            g.wait_ge(S["bias_rows"], 16 * L)
            for c in range(LC):
                n = min(32, L - 32 * c)
                for j in range(HG):
                    g.dma_start(negbias[32 * j:32 * j + n, :, c, :],
                                bscr[32 * c:32 * c + n, j:j + HG + 1:HG, :]).then_inc(S["bias_in"], 16)
            if both < B * CT:
                with g.Fori(both, B * CT) as u:
                    sum_rows(u)
            g.wait_ge(S["m_done"], 1)
            for i in range(2):
                g.memset(xw[i][:, :, 2 * L:QN], 0.0).then_inc(S["setup_pool"], 1)
            g.wait_ge(S["setup_pool"], 8)
            with g.Fori(0, B) as b:
                with strips(g) as s:
                    n = b * NS + s

                    def windows(p):
                        if p >= 2:
                            wait_apart(g, (S["piece"], n * 24 + 6 * (p - 1)))
                        for ct in range(CT):
                            last = g.tensor_copy(
                                xw[p % 2][:, ct, 0:2 * L].rearrange("p (v h w) -> p v h w", v=2, w=WS),
                                xs[:, ct, 1:WS + 1, 2 * WS * p:2 * WS * (p + 1)]
                                .rearrange("p h (v w) -> p v h w", v=2))
                        last.then_inc(S["xw_ready"], 1)

                    def block_diagonal(t):
                        p, v, hg = t // 4, t // 2 % 2, t % 2
                        g.wait_ge(S["piece_out"], n * 24 + 6 * p + hg + 1)
                        if t >= 2:
                            g.wait_ge(S["scores"], n * NT + t - 1)
                        q = q_sb[p % 2][:, hg, L * v:L * v + 32 * LC].rearrange("p (c i) -> p c i", i=32)
                        g.tensor_tensor(qbd[t % 2], q.unsqueeze(2).broadcast_to([128, LC, HG, 32]),
                                        block1[:].unsqueeze(1).broadcast_to([128, LC, HG, 32]),
                                        ALU.mult).then_inc(S["qbd_ready"], 1)

                    def normalise(t):
                        g.wait_ge(S["rden_ready"], n * NT + t + 1)
                        g.tensor_tensor(sp[t % 4], sp[t % 4], rden[t % 4].unsqueeze(2).broadcast_to([128, LC, L]),
                                        ALU.mult).then_inc(S["norm_done"], 1)

                    wait_apart(g, (S["xs_in"], n * 48 + 48))
                    windows(0)
                    windows(1)
                    for t in range(4):
                        block_diagonal(t)
                    normalise(0)
                    for t in range(NT):
                        if t % 4 == 1 and t // 4 + 2 < NP:
                            windows(t // 4 + 2)
                        if t + 4 < NT:
                            block_diagonal(t + 4)
                        if t + 1 < NT:
                            normalise(t + 1)
                    g.wait_ge(S["norm_done"], n * NT + NT)
                    g.tensor_tensor(tick[:, 0:1], tick[:, 3:4], tick[:, 3:4], ALU.add).then_inc(S["strip_done"], 1)
                    g.wait_ge(S["strip_done"], n * 4 + 4)
                with g.Fori(0, NCH // 2) as i:
                    for par in range(2):
                        g.wait_ge(S["abs_ready"], b * NCH + i * 2 + par + 1)
                        g.tensor_tensor(tg[par][0:96], tg[par][0:96],
                                        msb[par][0:96].unsqueeze(2).broadcast_to([96, 4, 96]),
                                        ALU.subtract).then_inc(S["tg_ready"], 1)
                for par in range(2):
                    g.wait_ge(S[f"y_out{par}"], b * (NG * 8) + NG * 8)
                g.wait_ge(S["agg_step"], b * 7 + 7)
            with g.Fori(0, B) as b:
                oi = out[bass.ds(b, 1)].rearrange("b (t p) n -> p (b t) n", p=128)
                for k in range(8):
                    g.wait_ge(f_gelu[k], b + 1)
                    g.dma_start(oi[:, k // 4, 2304 * (k % 4):2304 * (k % 4 + 1)], fb[k]).then_inc(f_out[k], 16)
            for k in range(8):
                g.wait_ge(f_out[k], 16 * B)

        @block.scalar
        def _(act):
            act.wait_ge(S["consts_in"], 16 * NCONST)
            with act.Fori(0, B * CT) as u:
                for q in range(32):
                    act.wait_ge(S["n_st1"], u * 32 + q + 1)
                    act.activation(NB1[:, 4 * q:4 * q + 4, :],
                                   ps[0:96, q % 3, 0:384].rearrange("p (c k) -> p c k", k=96),
                                   ACT.Copy).then_inc(S["n_b1"], 1)
                for kk in range(24):
                    act.wait_ge(S["n_st2"], u * 24 + kk + 1)
                    act.activation(NF[:, 4 * kk:4 * kk + 4, :],
                                   ps[:, 3 + kk % 4, 0:384].rearrange("p (c k) -> p c k", k=96),
                                   ACT.Abs).then_inc(S["n_f"], 1)
            act.wait_ge(S["m_conv"], 1)
            for b in range(B):
                act.activation(cmap[0:96, b, :], ps[0:96, b // 4, 96 * (b % 4):96 * (b % 4) + 96],
                               ACT.Copy).then_inc(S["m_cmap"], 1)
            act.wait_ge(S["m_sqrt_in"], 1)
            act.activation(sc[0:96, 12:13], sc[0:96, 11:12], ACT.Sqrt).then_inc(S["m_sqrt"], 1)
            act.wait_ge(S["m_ab"], 1)
            for b in range(B):
                act.activation(le[0:96, b, :], cmap[0:96, b, :], ACT.Relu, bias=sc[0:96, 14:15],
                               scale=sc[0:96, 13:14], accum_out=accb[0:96, b:b + 1]).then_inc(S["m_le"], 1)
            act.wait_ge(S["m_pool"], 1)
            act.activation(ngb[0:96], ps[0:96, 4, 0:B], ACT.Sigmoid, bias=sc[0:96, 3:4],
                           scale=sc[0:96, 16:17]).then_inc(S["m_ng"], 1)
            act.wait_ge(S["m_le"], B)
            act.activation(le[0:96], le[0:96], ACT.Sigmoid, scale=-1.0, bias=1.0).then_inc(S["m_sig"], 1)
            act.wait_ge(S["m_done"], 1)

            with act.Fori(0, B) as b:
                with strips(act) as s:
                    n = b * NS + s

                    def piece_out(i):
                        p, k = i // 6, i % 6
                        act.wait_ge(S["piece"], n * 24 + i + 1)
                        if k < 2:
                            if p >= 2:
                                act.wait_ge(S["qbd_ready"], n * NT + 4 * (p - 1))
                            o = act.activation(q_sb[p % 2][:, k, :], ps[:, psM, 0:QN], ACT.Identity,
                                               bias=nqb[:, k:k + 1], scale=-SCALE)
                        elif k < 4:
                            if p >= 2:
                                act.wait_ge(S["scores"], n * NT + 4 * (p - 1))
                            o = act.activation(k_sb[p % 2][:, k - 2, :], ps[:, psM, 0:2 * L], ACT.Identity,
                                               bias=qb[:, k:k + 1])
                        else:
                            if p >= 2:
                                act.wait_ge(S["av"], n * NT + 4 * (p - 1))
                            o = act.activation(v_sb[p % 2][0:HL, k - 4],
                                               ps[0:HL, psM, :].rearrange("p (f c) -> p f c", f=2), ACT.Copy)
                        o.then_inc(S["piece_out"], 1)

                    def exps(t):
                        for c in range(LC):
                            act.wait_ge(S["sb_ready"], n * 80 + LC * t + c + 1)
                            o = act.activation(sp[t % 4][:, c, :], sp[t % 4][:, c, :], ACT.Exp, scale=-1.0,
                                               bias=mn[t % 4][:, c:c + 1], accum_out=den[t % 4][:, c:c + 1])
                        o.then_inc(S["exp_done"], 1)

                    def pt_out(t):
                        act.wait_ge(S["ptrans"], n * 48 + 3 * t + 1)
                        if t >= 2:
                            act.wait_ge(S["av"], n * NT + t - 1)
                        act.activation(pt[t % 2][0:HL, 0:2].rearrange("p c f i -> p (c f i)"),
                                       ps[0:HL, psT[3 * t % 2], :], ACT.Copy).then_inc(S["pt_a"], 1)

                    def o_out(t):
                        p, v, hg = t // 4, t // 2 % 2, t % 2
                        w0 = 2 * WS * p + WS * v
                        act.wait_ge(S["av"], n * NT + t + 1)
                        act.activation(ostrip[:, hg, :, w0:w0 + WS],
                                       ps[:, psO, 0:L].rearrange("p (h w) -> p h w", w=WS), ACT.Identity,
                                       bias=qb[:, 4 + hg:5 + hg]).then_inc(S["o_out"], 1)

                    for i in range(6):
                        piece_out(i)
                    exps(0)
                    exps(1)
                    for t in range(NT):
                        if t >= 2:
                            o_out(t - 2)
                        if t + 2 < NT:
                            exps(t + 2)
                        made = pieces_at(t)
                        for i in made[:-1]:
                            piece_out(i)
                        pt_out(t)
                        for i in made[-1:]:
                            piece_out(i)
                    o_out(NT - 2)
                    o_out(NT - 1)
                    act.wait_ge(S["o_out"], n * NT + NT)
                    act.activation(tick[:, 1:2], tick[:, 3:4], ACT.Copy).then_inc(S["strip_done"], 1)
                    act.wait_ge(S["strip_done"], n * 4 + 4)

                def b1_out(q, par):
                    act.wait_ge(S["f1"], b * NCH + q + 1)
                    act.activation(b1[par][0:96], ps[0:96, par, 0:388].rearrange("p (c l) -> p c l", l=97),
                                   ACT.Copy).then_inc(S["b1_ready"], 1)

                def gate(q, par):
                    act.wait_ge(S["tg_ready"], b * NCH + q + 1)
                    act.activation(tg[par][0:96], tg[par][0:96], ACT.Sigmoid, scale=5.0).then_inc(S["gate_ready"], 1)

                def h_out(q, par):
                    act.wait_ge(S["i1"], b * NCH + q + 1)
                    act.activation(A[:, bass.ds(q * 4, 4), :],
                                   ps[0:96, 4 + par, 0:384].rearrange("p (c h) -> p c h", h=96),
                                   ACT.Copy).then_inc(S["h_ready"], 1)

                b1_out(0, 0)
                b1_out(1, 1)
                b1_out(2, 0)
                gate(0, 0)
                with act.Fori(0, NCH // 2 - 2) as i:
                    for par in (1, 0):
                        q = i * 2 + (1 if par else 2)
                        b1_out(q + 2, par)
                        gate(q, par)
                        h_out(q - 1, 1 - par)
                for q in range(NCH - 3, NCH):
                    if q + 2 < NCH:
                        b1_out(q + 2, q % 2)
                    gate(q, q % 2)
                    h_out(q - 1, 1 - q % 2)
                h_out(NCH - 1, (NCH - 1) % 2)

                def y_out(g_, par, free):
                    act.wait_ge(S["yps"], b * NG + g_ + 1)
                    if free:
                        act.wait_ge(S[f"y_out{par}"], b * (NG * 8) + (g_ - par) * 8)
                    act.activation(ys[par], ps[:, 4 + 2 * par:6 + 2 * par, 0:384], ACT.Copy).then_inc(S["y_ready"], 1)

                for par in range(2):
                    y_out(par, par, False)
                with act.Fori(1, NG // 2) as i:
                    for par in range(2):
                        y_out(i * 2 + par, par, True)
                for par in range(2):
                    act.wait_ge(S[f"y_out{par}"], b * (NG * 8) + NG * 8)
                act.wait_ge(S["agg_step"], b * 7 + 7)

            act.wait_ge(S["bnf_sqrt_in"], 1)
            act.activation(bn2s[:, 3, :], bn2s[:, 2, :], ACT.Sqrt).then_inc(S["bnf_sqrt"], 1)
            act.wait_ge(S["bnf_ready"], 1)
            with act.Fori(0, B) as b:
                for k in range(8):
                    act.wait_ge(f_in[k], b * 16 + 16)
                    act.activation(fb[k], fb[k], ACT.Gelu, scale=bn2s[:, 4, k // 4:k // 4 + 1],
                                   bias=bn2s[:, 5, k // 4:k // 4 + 1]).then_inc(f_gelu[k], 1)

        @block.vector
        def _(v):
            v.wait_ge(S["consts_in"], 16 * NCONST)
            v.tensor_scalar(nqb[:], qb[:, 0:CT], -SCALE, None, ALU.mult).then_inc(S["setup_vec"], 1)
            v.wait_ge(S["setup_pool"], 6)

            with v.Fori(0, B) as b:
                for ct in range(CT):
                    u = b * CT + ct
                    base = u * 8
                    for kk in range(24):
                        v.wait_ge(S["n_f"], u * 24 + kk + 1)
                        v.tensor_reduce(mm[:, 0, kk:kk + 1], NF[:, 4 * kk:4 * kk + 4, :], AX.XY, ALU.max)
                        last = v.tensor_reduce(mm[:, 1, kk:kk + 1], NF[:, 4 * kk:4 * kk + 4, :], AX.XY, ALU.min)
                    last.then_inc(S["n_chain"], 1)
                    v.wait_ge(S["n_chain"], base + 1)
                    v.tensor_reduce(mx[:, 0:1], mm[:, 0, :], AX.X, ALU.max).then_inc(S["n_chain"], 1)
                    v.tensor_reduce(mx[:, 1:2], mm[:, 1, :], AX.X, ALU.min).then_inc(S["n_chain"], 1)
                    v.wait_ge(S["n_chain"], base + 2)
                    v.tensor_scalar(mx[:, 2:3], mx[:, 0:1], 1e-6, None, ALU.add).then_inc(S["n_chain"], 1)
                    v.wait_ge(S["n_chain"], base + 4)
                    v.reciprocal(mx[:, 2:3], mx[:, 2:3]).then_inc(S["n_chain"], 1)
                    v.wait_ge(S["n_chain"], base + 5)
                    v.tensor_copy(rrep, mx[:, 2:3].broadcast_to([128, 32])).then_inc(S["n_r"], 1)
                    v.wait_ge(S["n_e"], u + 1)
                    v.tensor_copy(mx[:, 3:4], ps[:, 7, 511:512]).then_inc(S["n_chain"], 1)
                    v.wait_ge(S["n_chain"], base + 6)
                    v.tensor_scalar(erows[:], ps[:, 3:8, :].rearrange("p n k -> p (n k)")[:, 0:2304], mx[:, 3:4], None,
                                    ALU.subtract).then_inc(S["n_erow"], 1)
                    v.wait_ge(S["n_emt"], u * 64 + 64)
                    v.wait_ge(S["n_erow"], u + 1)
                    v.tensor_copy(tick[:, 2:3], tick[:, 3:4]).then_inc(S["n_free"], 1)
                    eb = esum[:, bass.ds(b, 1), :].rearrange("p b l -> p (b l)")
                    if ct == 0:
                        v.tensor_copy(eb, emt).then_inc(S["n_chain"], 1)
                    else:
                        v.wait_ge(S["n_chain"], base - 1)
                        v.tensor_tensor(eb, eb, emt, ALU.add).then_inc(S["n_chain"], 1)
                    v.wait_ge(S["n_chain"], base + 7)
                    v.tensor_copy(mx[:, 0:1], mx[:, 2:3]).then_inc(S["n_chain"], 1)
                    v.wait_ge(S["n_chain"], base + 8)
            v.wait_ge(S["taps_in"], 16 * NTAPS)
            m = [0]

            def link(ins):
                m[0] += 1
                ins.then_inc(S["m_chain"], 1)
                v.wait_ge(S["m_chain"], m[0])

            v.tensor_scalar(esum[:], esum[:], 1.0 / C, None, ALU.mult).then_inc(S["n_ec"], 1)
            v.wait_ge(S["n_et"], 1)
            for b in range(B):
                last = v.tensor_copy(emap[:, b, 1:97], ps[0:96, 4 + b // 4, 96 * (b % 4):96 * (b % 4) + 96])
            link(last)
            for d in range(3):
                link(v.tensor_scalar(band[0:96, d], shift[0:96, 0], taps[0:96, 3 * d:3 * d + 1], None, ALU.mult))
                for e in (1, 2):
                    link(v.scalar_tensor_tensor(band[0:96, d], shift[0:96, e], taps[0:96, 3 * d + e:3 * d + e + 1],
                                                band[0:96, d], ALU.mult, ALU.add))
            v.tensor_scalar(sc[0:96, 16:17], sc[0:96, 2:3], 1.0 / W, None, ALU.mult).then_inc(S["m_band"], 1)
            v.wait_ge(S["m_cmap"], B)
            for b in range(B):
                last = v.bn_stats(st6[0:96, b], cmap[0:96, b])
            link(last)
            link(v.bn_aggr(sc[0:96, 5:7], st6[0:96].rearrange("p b s -> p (b s)")))
            v.tensor_copy(sc[0:96, 7:8], sc[0:96, 5:6]).then_inc(S["m_mean_in"], 1)
            v.wait_ge(S["m_mean"], 1)
            link(v.tensor_copy(sc[0:96, 8:9], ps[0:96, 2, 0:1]))
            link(v.tensor_tensor(sc[0:96, 9:10], sc[0:96, 5:6], sc[0:96, 8:9], ALU.subtract))
            link(v.tensor_tensor(sc[0:96, 9:10], sc[0:96, 9:10], sc[0:96, 9:10], ALU.mult))
            v.tensor_tensor(sc[0:96, 10:11], sc[0:96, 9:10], sc[0:96, 6:7], ALU.add).then_inc(S["m_var_in"], 1)
            v.wait_ge(S["m_var"], 1)
            link(v.tensor_scalar(sc[0:96, 11:12], ps[0:96, 3, 0:1], 1e-5, None, ALU.add))
            v.reciprocal(sc[0:96, 11:12], sc[0:96, 11:12]).then_inc(S["m_sqrt_in"], 1)
            v.wait_ge(S["m_sqrt"], 1)
            link(v.tensor_tensor(sc[0:96, 13:14], sc[0:96, 12:13], sc[0:96, 0:1], ALU.mult))
            link(v.tensor_tensor(sc[0:96, 15:16], sc[0:96, 8:9], sc[0:96, 13:14], ALU.mult))
            v.tensor_tensor(sc[0:96, 14:15], sc[0:96, 1:2], sc[0:96, 15:16], ALU.subtract).then_inc(S["m_ab"], 1)
            v.wait_ge(S["m_ng"], 1)
            link(v.tensor_scalar(ngb[0:96], ngb[0:96], sc[0:96, 4:5], None, ALU.mult))
            v.wait_ge(S["m_sig"], 1)
            v.tensor_tensor(mask[:], le[0:96], ngb[0:96].unsqueeze(2).broadcast_to([96, B, 96]),
                            ALU.mult).then_inc(S["m_done"], 1)
            v.wait_ge(S["bias_in"], 16 * NBIAS)
            v.tensor_scalar(negbias[:], negbias[:], -1.0, None, ALU.mult).then_inc(S["setup_vec"], 1)
            v.wait_ge(S["setup_vec"], 2)
            v.wait_ge(S["m_done"], 1)

            with v.Fori(0, B) as b:
                with strips(v) as s:
                    n = b * NS + s

                    def scores_out(t):
                        waits = [(S["scores"], n * NT + t + 1)]
                        if t >= 4:
                            waits.append((S["ptrans"], n * 48 + 3 * (t - 3)))
                        wait_apart(v, *waits)
                        for c in range(LC):
                            v.tensor_tensor_reduce(
                                out=sp[t % 4][:, c, :], in0=psS[t % 2][:, c // 3, L * (c % 3):L * (c % 3) + L],
                                in1=negbias[:, t % 2, c, :], scale=1.0, scalar=BIG, op0=ALU.add, op1=ALU.min,
                                accum_out=mn[t % 4][:, c:c + 1]).then_inc(S["sb_ready"], 1)

                    def recip(t):
                        v.wait_ge(S["exp_done"], n * NT + t + 1)
                        v.reciprocal(rden[t % 4], den[t % 4]).then_inc(S["rden_ready"], 1)

                    def pt_out(t):
                        for un in (1, 2):
                            v.wait_ge(S["ptrans"], n * 48 + 3 * t + un + 1)
                            if un == 1 and t >= 2:
                                v.wait_ge(S["av"], n * NT + t - 1)
                            w = 512 if un == 1 else 256
                            v.tensor_copy(pt[t % 2][0:HL, 2 * un:2 * un + w // 256].rearrange("p c f i -> p (c f i)"),
                                          ps[0:HL, psT[(3 * t + un) % 2], 0:w]).then_inc(S["pt_d"], 1)

                    taps_order = [4, 0, 1, 2, 3, 5, 6, 7, 8]

                    def lpe_step(k):
                        ct, tap = k % 2, taps_order[k // 2]
                        dy, dx = tap // 3, tap % 3
                        if k == 0:
                            v.wait_ge(S["xs_in"], n * 48 + 48)
                        if tap == 4:
                            v.tensor_scalar(lpe[:, ct], xs[:, ct, 1:WS + 1, :], lw[:, ct, 4:5], lb[:, ct:ct + 1],
                                            ALU.mult, ALU.add).then_inc(S["lpe_step"], 1)
                            return
                        v.wait_ge(S["lpe_step"], n * 18 + k - 1)
                        w0, w1 = max(0, 1 - dx), min(W, W + 1 - dx)
                        v.scalar_tensor_tensor(lpe[:, ct, :, w0:w1], xs[:, ct, dy:dy + WS, w0 + dx - 1:w1 + dx - 1],
                                               lw[:, ct, tap:tap + 1], lpe[:, ct, :, w0:w1],
                                               ALU.mult, ALU.add).then_inc(S["lpe_step"], 1)

                    v.tensor_copy(mrow[0:96], mask[:, bass.ds(b, 1), bass.ds(s * WS, WS)]
                                  .rearrange("p b h -> p (b h)")).then_inc(S["mrow_ready"], 1)
                    for t in range(3):
                        scores_out(t)
                    recip(0)
                    recip(1)
                    for t in range(NT):
                        if t + 3 < NT:
                            scores_out(t + 3)
                        if t + 2 < NT:
                            recip(t + 2)
                        pt_out(t)
                        for k in range(18 * t // NT, 18 * (t + 1) // NT):
                            lpe_step(k)
                    v.wait_ge(S["mrow_ready"], n + 1)
                    for r in range(WS):
                        v.wait_ge(S["row_ps"], n * WS + r + 1)
                        rp = ps[0:96, r % 4, :]
                        v.scalar_tensor_tensor(rowt[r % 2][0:96], rp[:, C:2 * C], mrow[0:96, r:r + 1], pb[:],
                                               ALU.mult, ALU.add).then_inc(S["row_mask"], 1)
                        v.wait_ge(S["row_mask"], n * WS + r + 1)
                        v.tensor_tensor(A[:, :, bass.ds(s * WS + r, 1)].rearrange("p c h -> p (c h)"), rp[:, 0:C],
                                        rowt[r % 2][0:96], ALU.add).then_inc(S["a_row"], 1)
                    v.wait_ge(S["a_row"], n * WS + WS)
                    v.tensor_copy(tick[:, 2:3], tick[:, 3:4]).then_inc(S["strip_done"], 1)
                    v.wait_ge(S["strip_done"], n * 4 + 4)

                def centre(q, par):
                    v.wait_ge(S["f2"], b * NCH + q + 1)
                    v.tensor_copy(msb[par][0:96], ps[0:96, 2 + par, 384:388])
                    v.tensor_scalar(tg[par][0:96].rearrange("p c l -> p (c l)").bitcast(U32),
                                    ps[0:96, 2 + par, 0:384].bitcast(U32), 0x7FFFFFFF, None,
                                    ALU.bitwise_and).then_inc(S["abs_ready"], 1)

                def gated(q, par):
                    v.wait_ge(S["gate_ready"], b * NCH + q + 1)
                    v.tensor_tensor(gs[par][0:96], ps[0:96, 2 + par, 0:384].rearrange("p (c l) -> p c l", l=96),
                                    tg[par][0:96], ALU.mult).then_inc(S["g_ready"], 1)

                centre(0, 0)
                with v.Fori(0, NCH // 2 - 1) as i:
                    for par in range(2):
                        q = i * 2 + par
                        centre(q + 1, 1 - par)
                        gated(q, par)
                centre(NCH - 1, 1)
                gated(NCH - 2, 0)
                gated(NCH - 1, 1)

                def z_out(g_, par):
                    v.wait_ge(S[f"xc_in{par}"], b * (NG * 8) + (g_ - par) * 8 + 16)
                    v.wait_ge(S["zps"], b * NG + g_ + 1)
                    v.tensor_tensor(zs[par], ps[:, 2 * par:2 * par + 2, 0:384], xc[par], ALU.add).then_inc(S["z_ready"], 1)

                def y_stats(g_, par):
                    v.wait_ge(S["y_ready"], b * NG + g_ + 1)
                    for ct in range(CT):
                        last = v.bn_stats(stats[:, ct, bass.ds(g_, 1), :].rearrange("p g s -> p (g s)"), ys[par][:, ct, :])
                    last.then_inc(S["stat"], 1)

                z_out(0, 0)
                with v.Fori(0, NG // 2 - 1) as i:
                    for par in range(2):
                        z_out(i * 2 + par + 1, 1 - par)
                        y_stats(i * 2 + par, par)
                z_out(NG - 1, 1)
                y_stats(NG - 2, 0)
                y_stats(NG - 1, 1)
                wait_apart(v, (S["stat"], b * NG + NG))
                base = b * 7
                for ct in range(CT):
                    v.bn_aggr(ag[:, ct, :], stats[:, ct].rearrange("p g s -> p (g s)")).then_inc(S["agg_step"], 1)
                v.wait_ge(S["agg_step"], base + 2)
                for ct in range(CT):
                    dst = agg[:, ct, bass.ds(b, 1), :].rearrange("p b s -> p (b s)")
                    v.tensor_copy(dst[:, 1:2], ag[:, ct, 0:1]).then_inc(S["agg_step"], 1)
                    v.tensor_scalar(dst[:, 2:3], ag[:, ct, 1:2], float(HW), None, ALU.mult).then_inc(S["agg_step"], 1)
                v.wait_ge(S["agg_step"], base + 6)
                v.tensor_copy(ag[:, 0, 0:1], ag[:, 0, 1:2]).then_inc(S["agg_step"], 1)
                for par in range(2):
                    v.wait_ge(S[f"y_out{par}"], b * (NG * 8) + NG * 8)
                v.wait_ge(S["agg_step"], base + 7)

            f = [0]

            def flink(ins):
                f[0] += 1
                ins.then_inc(S["bnf_step"], 1)
                v.wait_ge(S["bnf_step"], f[0])

            flink(v.memset(agg[:, :, :, 0:1], float(HW)))
            for ct in range(CT):
                flink(v.bn_aggr(bn2s[:, 0:2, ct], agg[:, ct].rearrange("p b s -> p (b s)")))
            flink(v.tensor_scalar(bn2s[:, 2, :], bn2s[:, 1, :], 1e-5, None, ALU.add))
            v.reciprocal(bn2s[:, 2, :], bn2s[:, 2, :]).then_inc(S["bnf_sqrt_in"], 1)
            v.wait_ge(S["bnf_sqrt"], 1)
            flink(v.tensor_tensor(bn2s[:, 4, :], bn2s[:, 3, :], bn2[:, 0, :], ALU.mult))
            flink(v.tensor_tensor(bn2s[:, 1, :], bn2s[:, 0, :], bn2s[:, 4, :], ALU.mult))
            v.tensor_tensor(bn2s[:, 5, :], bn2[:, 1, :], bn2s[:, 1, :], ALU.subtract).then_inc(S["bnf_ready"], 1)

        @block.tensor
        def _(pe):
            def mmul(o, l, r, start=True, stop=True):
                return nc.tensor.matmul(o, l, r, start=start, stop=stop)

            pe.wait_ge(S["consts_in"], 16 * NCONST)
            pe.wait_ge(S["setup_pool"], 6)
            with pe.Fori(0, B * CT) as u:
                for q in range(32):
                    g = q // 4
                    if q % 4 == 0:
                        pe.wait_ge(n_x[g], u * 16 + 16)
                    if q >= 3:
                        pe.wait_ge(S["n_b1"], u * 32 + q - 2)
                    for i in range(4):
                        last = mmul(ps[0:96, q % 3, 96 * i:96 * i + 96], xg[g][0:96, 4 * (q % 4) + i, :],
                                    dct[:, 0:96])
                    last.then_inc(S["n_st1"], 1)
                pe.wait_ge(S["n_b1"], u * 32 + 32)
                pe.wait_ge(S["n_free"], u + 1)
                for kk in range(24):
                    if kk >= 4:
                        pe.wait_ge(S["n_f"], u * 24 + kk - 3)
                    for i in range(4):
                        last = mmul(ps[:, 3 + kk % 4, 96 * i:96 * i + 96], NB1[:, :, 4 * kk + i], dct[:, 0:96])
                    last.then_inc(S["n_st2"], 1)
                pe.wait_ge(S["n_f"], u * 24 + 24)
                pe.wait_ge(S["n_r"], u + 1)
                flat = NF.rearrange("p k l -> p (k l)")
                for n in range(5):
                    w = min(512, 2304 - 512 * n)
                    for j in range(4):
                        mmul(ps[32 * j:32 * j + 32, 3 + n, 0:w], rrep, flat[:, 2304 * j + 512 * n:2304 * j + 512 * n + w])
                for j in range(4):
                    last = mmul(ps[32 * j:32 * j + 32, 7, 511:512], rrep, mx[:, 1:2])
                last.then_inc(S["n_e"], 1)
            pe.wait_ge(S["n_ec"], 1)
            for b in range(B):
                last = nc.tensor.transpose(ps[0:96, 4 + b // 4, 96 * (b % 4):96 * (b % 4) + 96], esum[:, b, :],
                                           eye[0:96, 0:96])
            last.then_inc(S["n_et"], 1)
            pe.wait_ge(S["m_band"], 1)
            for g in range(0, B, 4):
                nb = min(4, B - g)
                for d in range(3):
                    last = mmul(ps[0:96, g // 4, 0:96 * nb], band[0:96, d], emap[:, g:g + nb, d:d + 96],
                                start=d == 0, stop=d == 2)
            last.then_inc(S["m_conv"], 1)
            pe.wait_ge(S["m_mean_in"], 1)
            mmul(ps[0:96, 2, 0:1], ones96[0:96], sc[0:96, 7:8]).then_inc(S["m_mean"], 1)
            pe.wait_ge(S["m_var_in"], 1)
            mmul(ps[0:96, 3, 0:1], ones96[0:96], sc[0:96, 10:11]).then_inc(S["m_var"], 1)
            pe.wait_ge(S["m_le"], B)
            mmul(ps[0:96, 4, 0:B], ones96[0:96], accb[0:96]).then_inc(S["m_pool"], 1)
            pe.wait_ge(S["m_done"], 1)
            pe.wait_ge(S["setup_vec"], 2)

            with pe.Fori(0, B) as b:
                with strips(pe) as s:
                    n = b * NS + s

                    def piece(i):
                        p, k = i // 6, i % 6
                        if k == 0:
                            pe.wait_ge(S["xw_ready"], n * NP + p + 1)
                        if i:
                            pe.wait_ge(S["piece_out"], n * 24 + i)
                        xp = xw[p % 2]
                        if k < 4:
                            w = QN if k < 2 else 2 * L
                            for kt in range(CT):
                                last = mmul(ps[:, psM, 0:w], wqkv[:, kt, 128 * k:128 * k + 128], xp[:, kt, 0:w],
                                            start=kt == 0, stop=kt == CT - 1)
                        else:
                            for f in range(2):
                                t0 = L * (k - 4) + HL * f
                                for kt in range(CT):
                                    last = mmul(ps[0:HL, psM, C * f:C * f + C], xp[:, kt, t0:t0 + HL],
                                                wqkv[:, kt, 2 * C:3 * C], start=kt == 0, stop=kt == CT - 1)
                        last.then_inc(S["piece"], 1)

                    def score(t):
                        p, v, hg = t // 4, t // 2 % 2, t % 2
                        pe.wait_ge(S["qbd_ready"], n * NT + t + 1)
                        pe.wait_ge(S["piece_out"], n * 24 + 6 * p + 3 + hg)
                        if t >= 2:
                            pe.wait_ge(S["sb_ready"], n * 80 + LC * (t - 1))
                        for c in range(LC):
                            last = mmul(psS[t % 2][:, c // 3, L * (c % 3):L * (c % 3) + L],
                                        qbd[t % 2][:, c].rearrange("p j i -> p (j i)"),
                                        k_sb[p % 2][:, hg, L * v:L * v + L])
                        last.then_inc(S["scores"], 1)

                    def transposes(t):
                        pe.wait_ge(S["norm_done"], n * NT + t + 1)
                        for un in range(3):
                            g = 3 * t + un
                            if g >= 2:
                                t0, u0 = (g - 2) // 3, (g - 2) % 3
                                if u0 == 0:
                                    pe.wait_ge(S["pt_a"], n * NT + t0 + 1)
                                else:
                                    pe.wait_ge(S["pt_d"], n * 2 * NT + 2 * t0 + u0)
                            for c in range(2 * un, min(2 * un + 2, LC)):
                                for f in range(2):
                                    at = ((c % 2) * 2 + f) * 128
                                    last = nc.tensor.transpose(ps[0:HL, psT[g % 2], at:at + 128],
                                                               sp[t % 4][:, c, HL * f:HL * f + HL], eye[:])
                            last.then_inc(S["ptrans"], 1)

                    def attend(t):
                        p, v, hg = t // 4, t // 2 % 2, t % 2
                        pe.wait_ge(S["pt_a"], n * NT + t + 1)
                        pe.wait_ge(S["pt_d"], n * 2 * NT + 2 * t + 2)
                        pe.wait_ge(S["piece_out"], n * 24 + 6 * p + 5 + v)
                        if t >= 1:
                            pe.wait_ge(S["o_out"], n * NT + t)
                        for f in range(2):
                            for j in range(HG):
                                ch = 128 * hg + 32 * j
                                last = mmul(ps[32 * j:32 * j + 32, psO, 0:32 * LC],
                                            v_sb[p % 2][0:HL, v, f, ch:ch + 32],
                                            pt[t % 2][0:HL, :, f, 32 * j:32 * j + 32], start=f == 0, stop=f == 1)
                        last.then_inc(S["av"], 1)

                    for i in range(6):
                        piece(i)
                    for t in range(3):
                        score(t)
                    for t in range(NT):
                        if t + 3 < NT:
                            score(t + 3)
                        made = pieces_at(t)
                        for i in made[:-1]:
                            piece(i)
                        transposes(t)
                        for i in made[-1:]:
                            piece(i)
                        if t >= 1:
                            attend(t - 1)
                    attend(NT - 1)
                    pe.wait_ge(S["o_out"], n * NT + NT)
                    pe.wait_ge(S["lpe_step"], n * 18 + 18)
                    for r in range(WS):
                        if r >= 4:
                            pe.wait_ge(S["a_row"], n * WS + r - 3)
                        for ct in range(CT):
                            nc.tensor.transpose(ps[0:96, r % 4, C + 128 * ct:C + 128 * ct + 128], lpe[:, ct, r, :], eye[:])
                        for ct in range(CT):
                            last = mmul(ps[0:96, r % 4, 0:C], ostrip[:, ct, r, :], wproj[:, ct, :],
                                        start=ct == 0, stop=ct == CT - 1)
                        last.then_inc(S["row_ps"], 1)
                    pe.wait_ge(S["a_row"], n * WS + WS)
                    mmul(ps[0:96, psM, 0:1], eye[:, 0:96], eye[:, 0:1]).then_inc(S["strip_done"], 1)
                    pe.wait_ge(S["strip_done"], n * 4 + 4)

                def f1(q):
                    if q >= 2:
                        pe.wait_ge(S["b1_ready"], b * NCH + q - 1)
                    for i in range(4):
                        last = mmul(ps[0:96, q % 2, 97 * i:97 * i + 97], A[:, 4 * q + i, :], dct[:])
                    last.then_inc(S["f1"], 1)

                def f2(q):
                    pe.wait_ge(S["b1_ready"], b * NCH + q + 1)
                    if q >= 2:
                        pe.wait_ge(S["g_ready"], b * NCH + q - 1)
                    mmul(ps[0:96, 2 + q % 2, 0:384], dct[:, 0:96], b1[q % 2][0:96, :, 0:96])
                    mmul(ps[0:96, 2 + q % 2, 384:388], meanm[:], b1[q % 2][0:96, :, 96]).then_inc(S["f2"], 1)

                def i1(q):
                    pe.wait_ge(S["g_ready"], b * NCH + q + 1)
                    if q >= 2:
                        pe.wait_ge(S["h_ready"], b * NCH + q - 1)
                    for i in range(4):
                        last = mmul(ps[0:96, 4 + q % 2, 96 * i:96 * i + 96], gs[q % 2][0:96, i, :], inv[:])
                    last.then_inc(S["i1"], 1)

                f1(0)
                f1(1)
                f2(0)
                for q in range(NCH):
                    if q + 2 < NCH:
                        f1(q + 2)
                    if q + 1 < NCH:
                        f2(q + 1)
                    if q >= 1:
                        i1(q - 1)
                i1(NCH - 1)
                pe.wait_ge(S["h_ready"], b * NCH + NCH)

                def zrows(g):
                    if g >= 2:
                        pe.wait_ge(S["z_ready"], b * NG + g - 1)
                    for ct in range(CT):
                        for i in range(4):
                            last = mmul(ps[:, 2 * (g % 2) + ct, 96 * i:96 * i + 96],
                                        A[:, 128 * ct:128 * ct + 128, 4 * g + i], inv[:])
                    last.then_inc(S["zps"], 1)

                def yrows(g):
                    pe.wait_ge(S["z_ready"], b * NG + g + 1)
                    if g >= 2:
                        pe.wait_ge(S["y_ready"], b * NG + g - 1)
                    for mt in range(CT):
                        for kt in range(CT):
                            last = mmul(ps[:, 4 + 2 * (g % 2) + mt, 0:384], wfr[:, kt, 128 * mt:128 * mt + 128],
                                        zs[g % 2][:, kt, :], start=kt == 0, stop=kt == CT - 1)
                    last.then_inc(S["yps"], 1)

                zrows(0)
                for g in range(NG):
                    if g + 1 < NG:
                        zrows(g + 1)
                    yrows(g)
                for par in range(2):
                    pe.wait_ge(S[f"y_out{par}"], b * (NG * 8) + NG * 8)
                pe.wait_ge(S["agg_step"], b * 7 + 7)


_NAMES = ("x", "wqkvT", "wprojT", "wfrT", "qkv_b", "proj_b", "lpe_w", "lpe_b", "lpe_scale", "rpb_rev", "ec_w",
          "bn1_g", "bn1_b", "nl_w", "nl_b", "bn2_g", "bn2_b")


def lay_out(inputs):
    p = "L0_conv_"
    g = {k.removeprefix(p): np.asarray(v) for k, v in inputs.items()}
    t = g["rpb_table"].T.reshape(HEADS, 2 * WS - 1, 2 * WS - 1)
    arrays = {
        "x": g["x"], "wqkvT": g["qkv_w"].T, "wprojT": g["proj_w"].T, "wfrT": g["fr_w"].reshape(C, C).T,
        "qkv_b": g["qkv_b"].reshape(-1, 128).T, "proj_b": g["proj_b"], "lpe_w": g["lpe_w"].reshape(C, 9), "lpe_b": g["lpe_b"].reshape(-1, 128).T,
        "lpe_scale": g["lpe_scale"], "rpb_rev": t[:, ::-1, ::-1], "ec_w": g["ec_w"].reshape(9),
        "bn1_g": g["bn1_g"], "bn1_b": g["bn1_b"], "nl_w": g["nl_w"].reshape(1), "nl_b": g["nl_b"],
        "bn2_g": g["bn2_g"].reshape(-1, 128).T, "bn2_b": g["bn2_b"].reshape(-1, 128).T,
    }
    arrays.update(shape_constants())
    return {k: np.ascontiguousarray(v) for k, v in arrays.items()}


def kernel(**inputs):
    import concourse.bacc as _bacc
    from concourse.bass_utils import run_bass_kernel_spmd as _run

    arrays = lay_out(inputs)
    B = arrays["x"].shape[0]
    nc = _bacc.Bacc("TRN2", target_bir_lowering=False, num_devices=1)
    aps = {k: nc.dram_tensor(f"in_{k}", v.shape, mybir.dt.from_np(v.dtype), kind="ExternalInput").ap()
           for k, v in arrays.items()}
    out = nc.dram_tensor("out_0", (B, C, HW), F32, kind="ExternalOutput").ap()
    build(nc, aps, out, B)
    r = _run(nc, [{f"in_{k}": v for k, v in arrays.items()}], core_ids=[0])
    return r.results[0]["out_0"].reshape(B, C, H, W)
```

```python
import math
from contextlib import ExitStack

import numpy as np
import concourse.bass as bass
from concourse import mybir
from concourse.alu_op_type import AluOpType as ALU

ACT = mybir.ActivationFunctionType
AX = mybir.AxisListType
F32 = mybir.dt.float32
U32 = mybir.dt.uint32

C, H, W = 256, 96, 96
HEADS, WS, HD = 8, 12, 32
L = WS * WS
HL = L // 2
CT = C // 128
HG = 4
LC = 5
QN = 2 * L + 16
NS = H // WS
NP = W // (2 * WS)
NT = NP * 4
SW = WS * W
SCALE = HD ** -0.5
NPC = 8
NCH = C // 4
NG = H // 4
HW = H * W
BIG = 3.0e38


def shape_constants():
    k = np.arange(96)
    cos = np.cos(np.pi * np.outer(2 * k + 1, k) / 192)
    dct = 2 * cos
    inv = np.where(k[:, None] == 0, 1.0, 2.0) * cos.T / 192
    inv[94] += math.cos(math.pi * 94 / 192) * (-1.0) ** k / 192
    rowsum = dct.sum(1)
    shifts = np.zeros((96, 3, 96))
    for d in range(3):
        for y in range(96):
            if 0 <= y + d - 1 < 96:
                shifts[y + d - 1, d, y] = 1
    blocks = np.zeros((128, HG, 32))
    for j in range(HG):
        blocks[32 * j:32 * j + 32, j] = 1
    f = lambda a: np.ascontiguousarray(a, np.float32)
    return {
        "c_dct": f(np.concatenate([dct, rowsum[:, None]], 1)),
        "c_mean": f(np.repeat(rowsum[:, None] / (96 * 96), 96, 1)),
        "c_inv": f(inv),
        "c_shift": f(shifts.reshape(96, 288)),
        "c_block": f(blocks.reshape(128, 128)),
        "c_eye": f(np.eye(128)),
        "c_zero": f(np.zeros((128, CT * W))),
    }


def build(nc, a, out, B):
    NSTRIP = B * NS
    yscr = nc.dram_tensor("y_scratch", [B, C, HW], F32, kind="Internal").ap()
    bscr = nc.dram_tensor("bias_scratch", [L, HEADS, L], F32, kind="Internal").ap()
    x = a["x"]

    with ExitStack() as ctx:
        def sb(name, shape):
            return ctx.enter_context(nc.sbuf_tensor(name, shape, F32))

        def sem(name):
            return ctx.enter_context(nc.semaphore(name))

        wqkv = sb("wqkv", [128, CT, 3 * C])
        wproj = sb("wproj", [128, CT, C])
        negbias = sb("negbias", [128, CT, LC, L])
        dct = sb("dct", [96, 97])
        meanm = sb("meanm", [96, 96])
        inv = sb("inv", [96, 96])
        block1 = sb("block1", [128, HG, 32])
        eye = sb("eye", [128, 128])
        qb = sb("qb", [128, 6])
        nqb = sb("nqb", [128, CT])
        pb = sb("pb", [96, C])
        lw = sb("lw", [128, CT, 9])
        lb = sb("lb", [128, CT])
        mask = sb("mask", [96, B, 96])
        agg = sb("agg", [128, CT, B, 3])
        bn2 = sb("bn2", [128, 2, CT])
        bn2s = sb("bn2s", [128, 6, CT])
        tick = sb("tick", [128, 4])
        AH = sb("AH", [128, C * 96])
        xs = [sb(f"xs{i}", [128, CT, WS + 2, W]) for i in range(2)]
        WORKN = 18056
        work = sb("work", [128, WORKN])
        used = {}

        def carve(phase, *shape):
            n = int(np.prod(shape))
            at = used.get(phase, 0)
            used[phase] = at + n
            assert at + n <= WORKN, (phase, at + n)
            v = work[:, at:at + n]
            names = "abcd"[:len(shape)]
            return v if len(shape) == 1 else v.rearrange(
                f"p ({' '.join(names)}) -> p {' '.join(names)}", **dict(zip(names[1:], shape[1:])))

        A = AH[0:96, :].rearrange("p (c h) -> p c h", h=96)
        xw = [carve("a", CT, 2 * L) for _ in range(2)]
        q_sb = [carve("a", CT, QN) for _ in range(2)]
        k_sb = [carve("a", CT, 2 * L) for _ in range(2)]
        vt = carve("a", CT, 2 * L)
        v_sb = [carve("a", 2, 2, C) for _ in range(2)]
        qbd = [carve("a", LC, HG, 32) for _ in range(2)]
        sp = [carve("a", LC, L) for _ in range(4)]
        pt = [carve("a", LC, 2, 128) for _ in range(2)]
        ostrip = carve("a", CT, WS, W)
        lpe = carve("a", CT, WS, W)
        mn = [carve("a", LC) for _ in range(4)]
        den = [carve("a", LC) for _ in range(4)]
        rden = [carve("a", LC) for _ in range(4)]
        mrow = carve("a", WS)
        rowt = [carve("a", C) for _ in range(2)]
        wfr = carve("f", CT, C)
        b1 = [carve("f", 4, 97) for _ in range(2)]
        tg = [carve("f", 4, 96) for _ in range(2)]
        gs = [carve("f", 4, 96) for _ in range(2)]
        msb = [carve("f", 4) for _ in range(2)]
        xc = [carve("f", CT, 384) for _ in range(2)]
        zs = [carve("f", CT, 384) for _ in range(2)]
        ys = [carve("f", CT, 384) for _ in range(2)]
        stats = carve("f", CT, NG, 6)
        ag = carve("f", CT, 2)
        xg = [carve("n", 16, 96) for _ in range(8)]
        mm = carve("n", 2, 24)
        mx = carve("n", 4)
        emap = AH[0:96, 96 * 256 - 98 * B:].rearrange("p (b k) -> p b k", b=B)
        erows = carve("n", 2304)
        emt = AH[0:96, 224 * 96:225 * 96]
        esum = AH[0:96, 225 * 96:(225 + B) * 96].rearrange("p (b l) -> p b l", b=B)
        rrep = carve("n", 32)
        shift = carve("n", 3, 96)
        taps = carve("n", 9)
        band = carve("n", 3, 96)
        cmap = carve("n", B, 96)
        le = carve("n", B, 96)
        sc = carve("n", 32)
        st6 = carve("n", B, 6)
        accb = carve("n", B)
        ngb = carve("n", B)
        ones = carve("n", 96)
        ones96 = carve("n", 96)
        NB1 = A[:, 0:128, :]
        NF = AH[:, 128 * 96:128 * 96 + 96 * 96].rearrange("p (k l) -> p k l", l=96)

        ps = ctx.enter_context(nc.psum_tensor("ps", [128, 8, 512], F32))
        psS = [ps[:, 0:2, :], ps[:, 2:4, :]]
        psT = [4, 5, 6]
        psO = ps[:, 6, 256:256 + 32 * LC]
        psM = 7

        S = {n: sem(n) for n in (
            "consts_in taps_in setup_vec setup_pool bias_rows bias_in "
            "n_st1 n_b1 n_st2 n_f n_chain n_r n_e n_free n_erow n_emt n_et n_ec "
            "m_band m_conv m_cmap m_chain m_mean_in m_mean m_var_in m_var m_sqrt_in m_sqrt m_ab m_le m_pool "
            "m_ng m_sig m_done "
            "wfr_in q_pad xs_in0 xs_in1 xw_ready piece piece_out qbd_ready scores sb_ready exp_done rden_ready norm_done "
            "ptrans pt_a pt_d av o_out lpe_step row_ps row_mask a_row mrow_ready image_done "
            "f1 b1_ready f2 abs_ready tg_ready gate_ready g_ready i1 h_ready xc_in0 xc_in1 zps z_ready yps y_ready "
            "stat y_out0 y_out1 agg_step "
            "bnf_step bnf_sqrt_in bnf_sqrt bnf_ready").split()}
        n_x = [sem(f"n_x{i}") for i in range(8)]
        f_in = [sem(f"f_in{i}") for i in range(8)]
        f_gelu = [sem(f"f_gelu{i}") for i in range(8)]
        f_out = [sem(f"f_out{i}") for i in range(8)]
        fb = [AH[:, 2304 * i:2304 * (i + 1)] for i in range(8)]
        NCONST, NTAPS, NBIAS = 14, 6, 4 * LC

        def bc(v, n):
            return v.rearrange("(a n) -> a n", a=1).broadcast_to([n, v.shape[0]])

        def wait_apart(eng, *waits):
            values = [v if isinstance(v, int) else eng.snap(v) for _, v in waits]
            for value in values:
                eng.compute_val(value)
            eng.wait_ge(S["consts_in"], 16 * NCONST)
            for (which, _), value in zip(waits, values):
                eng.wait_ge(which, value)

        def pieces_at(t, last):
            p, k = (t + 1) // 4 + 1, (t + 1) % 4
            return [] if last and p >= NP else [NPC * p + 2 * k, NPC * p + 2 * k + 1]

        def each_strip(eng, strip):
            with eng.Fori(0, NS - 1) as s:
                strip(s, False)
            strip(NS - 1, True)

        def each_strip_by_parity(eng, strip):
            with eng.Fori(0, NS // 2 - 1) as i:
                strip(i * 2, 0, False)
                strip(i * 2 + 1, 1, False)
            strip(NS - 2, 0, False)
            strip(NS - 1, 1, True)

        block = ctx.enter_context(nc.Block())

        @block.sync
        def _(sy):
            for dst, src in (
                (wqkv[:], a["wqkvT"].rearrange("(t p) n -> p t n", p=128)),
                (wproj[:], a["wprojT"].rearrange("(t p) n -> p t n", p=128)),
                (dct[:], a["c_dct"]), (meanm[:], a["c_mean"]), (inv[:], a["c_inv"]),
                (block1[:].rearrange("p a b -> p (a b)"), a["c_block"]), (eye[:], a["c_eye"]),
                (qb[:], a["qkv_b"]),
                (pb[:], bc(a["proj_b"], 96)),
                (lw[:], a["lpe_w"].rearrange("(t p) n -> p t n", p=128)),
                (lb[:], a["lpe_b"]),
                (bn2[:, 0, :], a["bn2_g"]),
                (bn2[:, 1, :], a["bn2_b"]),
                (shift[0:96], a["c_shift"].rearrange("p (a b) -> p a b", a=3)),
            ):
                sy.dma_start(dst, src).then_inc(S["consts_in"], 16)
            for dst, src in ((taps[0:96], a["ec_w"]), (sc[0:96, 0:1], a["bn1_g"]), (sc[0:96, 1:2], a["bn1_b"]),
                             (sc[0:96, 2:3], a["nl_w"]), (sc[0:96, 3:4], a["nl_b"]), (sc[0:96, 4:5], a["lpe_scale"])):
                sy.dma_start(dst, bc(src, 96)).then_inc(S["taps_in"], 16)

            def load_units(b, first):
                for ct in range(CT):
                    u = b * CT + ct
                    for g in range(8):
                        if not first or ct:
                            sy.wait_ge(S["n_st1"], u * 32 + 4 * (g + 1) - 32)
                        sy.dma_start(xg[g][0:96],
                                     x[bass.ds(b, 1), ct * 128 + 16 * g:ct * 128 + 16 * g + 16]
                                     .rearrange("b c h w -> h (b c) w")).then_inc(n_x[g], 16)
            load_units(0, True)
            if B > 1:
                with sy.Fori(1, B) as b:
                    load_units(b, False)

            def load_strip(b, s, par, where):
                xi = x[bass.ds(b, 1)].rearrange("b (t p) h w -> p (b t) h w", p=128)
                rows = [(0, s * WS - 1, 1), (1, s * WS, WS), (WS + 1, s * WS + WS, 1)]
                for at, r0, n in rows:
                    if (where == "top" and at == 0) or (where == "bottom" and at == WS + 1):
                        src = a["c_zero"].rearrange("p (t h w) -> p t h w", t=CT, h=1)
                        n = 1
                    else:
                        src = xi[:, :, bass.ds(r0, n), :]
                    sy.dma_start(xs[par][:, :, at:at + n, :], src).then_inc(S[f"xs_in{par}"], 16)

            def after_strip(b, s):
                n = b * NS + s
                wait_apart(sy, (S["xw_ready"], n * NP - NP), (S["lpe_step"], n * 18 - 18))

            load_strip(0, 0, 0, "top")
            load_strip(0, 1, 1, "inner")
            sy.wait_ge(S["m_done"], 1)

            def image(b, last):
                with sy.Fori(1, NS // 2 - 1) as i:
                    for par in range(2):
                        after_strip(b, i * 2 + par)
                        load_strip(b, i * 2 + par, par, "inner")
                for par, where in enumerate(("inner", "bottom")):
                    after_strip(b, NS - 2 + par)
                    load_strip(b, NS - 2 + par, par, where)
                wait_apart(sy, (S["image_done"], b * 4 + 4))
                sy.dma_start(wfr, a["wfrT"].rearrange("(t p) n -> p t n", p=128)).then_inc(S["wfr_in"], 16)
                if not last:
                    load_strip(b + 1, 0, 0, "top")
                    load_strip(b + 1, 1, 1, "inner")
                xi = x[bass.ds(b, 1)].rearrange("b (t p) h w -> p (b t) (h w)", p=128)
                yi = yscr[bass.ds(b, 1)].rearrange("b (t p) n -> p (b t) n", p=128)

                def load_x(g, par):
                    sy.dma_start(xc[par], xi[:, :, bass.ds(g * 384, 384)]).then_inc(S[f"xc_in{par}"], 16)

                def store_y(g, par):
                    wait_apart(sy, (S["y_ready"], b * NG + g + 1))
                    sy.dma_start(yi[:, :, bass.ds(g * 384, 384)], ys[par]).then_inc(S[f"y_out{par}"], 16)

                load_x(0, 0)
                load_x(1, 1)
                with sy.Fori(0, NG // 2 - 1) as i:
                    for par in range(2):
                        wait_apart(sy, (S["z_ready"], b * NG + i * 2 + par + 1))
                        load_x(i * 2 + 2 + par, par)
                        store_y(i * 2 + par, par)
                for par in range(2):
                    store_y(NG - 2 + par, par)
                wait_apart(sy, *[(S[f"y_out{par}"], b * (NG * 8) + NG * 8) for par in range(2)],
                           (S["agg_step"], b * 7 + 7))

            if B > 1:
                with sy.Fori(0, B - 1) as b:
                    image(b, False)
            image(B - 1, True)

            def load_f(b, first):
                yi = yscr[bass.ds(b, 1)].rearrange("b (t p) n -> p (b t) n", p=128)
                for k in range(8):
                    if not first:
                        sy.wait_ge(f_out[k], b * 16)
                    sy.dma_start(fb[k], yi[:, k // 4, 2304 * (k % 4):2304 * (k % 4 + 1)]).then_inc(f_in[k], 16)
            load_f(0, True)
            if B > 1:
                with sy.Fori(1, B) as b:
                    load_f(b, False)

        @block.gpsimd
        def _(g):
            g.memset(negbias[:], 0.0).then_inc(S["setup_pool"], 1)
            g.memset(emap, 0.0).then_inc(S["setup_pool"], 1)
            g.memset(ones, 1.0).then_inc(S["setup_pool"], 1)
            g.memset(ones96[0:96], 1.0 / 96).then_inc(S["setup_pool"], 1)
            g.memset(tick[:, 3:4], 0.0).then_inc(S["setup_pool"], 1)
            g.memset(tick[:, 0:1], 0.0).then_inc(S["n_free"], 1)
            g.wait_ge(S["setup_pool"], 5)
            tab = a["rpb_rev"]

            def sum_rows(u):
                wait_apart(g, (S["n_erow"], u + 1))
                for j in range(4):
                    g.dma_start(emt[24 * j:24 * j + 24, :], erows[32 * j:32 * j + 1, :]
                                .rearrange("p (k l) -> p k l", l=96)).then_inc(S["n_emt"], 16)

            def bias_rows(r):
                with g.Fori(0, WS) as c:
                    g.dma_start(bscr[bass.ds(r * WS + c, 1)].rearrange("a h (y x) -> (a h) y x", y=WS),
                                tab[:, bass.ds(r * -1 + (WS - 1), WS), bass.ds(c * -1 + (WS - 1), WS)]
                                ).then_inc(S["bias_rows"], 16)

            both = min(WS, B * CT)
            with g.Fori(0, both) as u:
                sum_rows(u)
                bias_rows(u)
            if both < WS:
                with g.Fori(both, WS) as r:
                    bias_rows(r)
            g.wait_ge(S["bias_rows"], 16 * L)
            for c in range(LC):
                n = min(32, L - 32 * c)
                for j in range(HG):
                    g.dma_start(negbias[32 * j:32 * j + n, :, c, :],
                                bscr[32 * c:32 * c + n, j:j + HG + 1:HG, :]).then_inc(S["bias_in"], 16)
            if both < B * CT:
                with g.Fori(both, B * CT) as u:
                    sum_rows(u)
            g.wait_ge(S["m_done"], 1)
            with g.Fori(0, B) as b:
                def strip(s, par, last, first=False):
                    n = b * NS + s

                    def windows(p):
                        src = xs[par if p < NP else 1 - par]
                        if p == NP:
                            wait_apart(g, (S[f"xs_in{1 - par}"], (n + par) * 24 + 48))
                        if p >= 2:
                            wait_apart(g, (S["piece"], (n * NP + p - 2) * NPC + 6))
                        for ct in range(CT):
                            last = g.tensor_copy(
                                xw[p % 2][:, ct, 0:2 * L].rearrange("p (v h w) -> p v h w", v=2, w=WS),
                                src[:, ct, 1:WS + 1, 2 * WS * (p % NP):2 * WS * (p % NP + 1)]
                                .rearrange("p h (v w) -> p v h w", v=2))
                        last.then_inc(S["xw_ready"], 1)

                    def block_diagonal(t):
                        p, v, hg = t // 4, t // 2 % 2, t % 2
                        g.wait_ge(S["piece_out"], (n * NP + p) * NPC + hg + 1)
                        if t >= 2:
                            g.wait_ge(S["scores"], n * NT + t - 1)
                        q = q_sb[p % 2][:, hg, L * v:L * v + 32 * LC].rearrange("p (c i) -> p c i", i=32)
                        g.tensor_tensor(qbd[t % 2], q.unsqueeze(2).broadcast_to([128, LC, HG, 32]),
                                        block1[:].unsqueeze(1).broadcast_to([128, LC, HG, 32]),
                                        ALU.mult).then_inc(S["qbd_ready"], 1)

                    def normalise(t):
                        g.wait_ge(S["rden_ready"], n * NT + t + 1)
                        g.tensor_tensor(sp[t % 4], sp[t % 4], rden[t % 4].unsqueeze(2).broadcast_to([128, LC, L]),
                                        ALU.mult).then_inc(S["norm_done"], 1)

                    if first:
                        wait_apart(g, (S["xs_in0"], n * 24 + 48))
                        windows(0)
                        windows(1)
                        for i in range(2):
                            g.memset(q_sb[i][:, :, 2 * L:QN], 0.0).then_inc(S["q_pad"], 1)
                        wait_apart(g, (S["q_pad"], b * 2 + 2))
                        for t in range(4):
                            block_diagonal(t)
                        normalise(0)
                        return
                    for t in range(NT):
                        if t % 4 == 1 and not (last and t // 4 + 2 >= NP):
                            windows(t // 4 + 2)
                        if not (last and t + 4 >= NT):
                            block_diagonal(t + 4)
                        if not (last and t + 1 >= NT):
                            normalise(t + 1)

                strip(0, 0, False, first=True)
                each_strip_by_parity(g, strip)
                g.wait_ge(S["norm_done"], b * (NS * NT) + NS * NT)
                g.tensor_tensor(tick[:, 0:1], tick[:, 3:4], tick[:, 3:4], ALU.add).then_inc(S["image_done"], 1)
                wait_apart(g, (S["image_done"], b * 4 + 4))
                with g.Fori(0, NCH // 2) as i:
                    for par in range(2):
                        g.wait_ge(S["abs_ready"], b * NCH + i * 2 + par + 1)
                        g.tensor_tensor(tg[par][0:96], tg[par][0:96],
                                        msb[par][0:96].unsqueeze(2).broadcast_to([96, 4, 96]),
                                        ALU.subtract).then_inc(S["tg_ready"], 1)
                for par in range(2):
                    g.wait_ge(S[f"y_out{par}"], b * (NG * 8) + NG * 8)
                g.wait_ge(S["agg_step"], b * 7 + 7)
            with g.Fori(0, B) as b:
                oi = out[bass.ds(b, 1)].rearrange("b (t p) n -> p (b t) n", p=128)
                for k in range(8):
                    g.wait_ge(f_gelu[k], b + 1)
                    g.dma_start(oi[:, k // 4, 2304 * (k % 4):2304 * (k % 4 + 1)], fb[k]).then_inc(f_out[k], 16)
            for k in range(8):
                g.wait_ge(f_out[k], 16 * B)

        @block.scalar
        def _(act):
            act.wait_ge(S["consts_in"], 16 * NCONST)
            with act.Fori(0, B * CT) as u:
                for q in range(32):
                    act.wait_ge(S["n_st1"], u * 32 + q + 1)
                    act.activation(NB1[:, 4 * q:4 * q + 4, :],
                                   ps[0:96, q % 3, 0:384].rearrange("p (c k) -> p c k", k=96),
                                   ACT.Copy).then_inc(S["n_b1"], 1)
                for kk in range(24):
                    act.wait_ge(S["n_st2"], u * 24 + kk + 1)
                    act.activation(NF[:, 4 * kk:4 * kk + 4, :],
                                   ps[:, 3 + kk % 4, 0:384].rearrange("p (c k) -> p c k", k=96),
                                   ACT.Abs).then_inc(S["n_f"], 1)
            act.wait_ge(S["m_conv"], 1)
            for b in range(B):
                act.activation(cmap[0:96, b, :], ps[0:96, b // 4, 96 * (b % 4):96 * (b % 4) + 96],
                               ACT.Copy).then_inc(S["m_cmap"], 1)
            act.wait_ge(S["m_sqrt_in"], 1)
            act.activation(sc[0:96, 12:13], sc[0:96, 11:12], ACT.Sqrt).then_inc(S["m_sqrt"], 1)
            act.wait_ge(S["m_ab"], 1)
            for b in range(B):
                act.activation(le[0:96, b, :], cmap[0:96, b, :], ACT.Relu, bias=sc[0:96, 14:15],
                               scale=sc[0:96, 13:14], accum_out=accb[0:96, b:b + 1]).then_inc(S["m_le"], 1)
            act.wait_ge(S["m_pool"], 1)
            act.activation(ngb[0:96], ps[0:96, 4, 0:B], ACT.Sigmoid, bias=sc[0:96, 3:4],
                           scale=sc[0:96, 16:17]).then_inc(S["m_ng"], 1)
            act.wait_ge(S["m_le"], B)
            act.activation(le[0:96], le[0:96], ACT.Sigmoid, scale=-1.0, bias=1.0).then_inc(S["m_sig"], 1)
            act.wait_ge(S["m_done"], 1)

            with act.Fori(0, B) as b:
                def strip(s, last, first=False):
                    n = b * NS + s

                    def piece_out(i):
                        p, k = i // NPC, i % NPC
                        act.wait_ge(S["piece"], n * (NP * NPC) + i + 1)
                        if k < 2:
                            if p >= 2:
                                act.wait_ge(S["qbd_ready"], n * NT + 4 * (p - 1))
                            o = act.activation(q_sb[p % 2][:, k, 0:2 * L], ps[:, psM, 0:2 * L], ACT.Identity,
                                               bias=nqb[:, k:k + 1], scale=-SCALE)
                        elif k < 4:
                            if p >= 2:
                                act.wait_ge(S["scores"], n * NT + 4 * (p - 1))
                            o = act.activation(k_sb[p % 2][:, k - 2, :], ps[:, psM, 0:2 * L], ACT.Identity,
                                               bias=qb[:, k:k + 1])
                        elif k < 6:
                            o = act.activation(vt[:, k - 4, :], ps[:, psM, 0:2 * L], ACT.Copy)
                        else:
                            if p >= 2:
                                act.wait_ge(S["av"], n * NT + 4 * (p - 1))
                            o = act.activation(v_sb[p % 2][0:HL, k - 6],
                                               ps[0:HL, psM, :].rearrange("p (f c) -> p f c", f=2), ACT.Copy)
                        o.then_inc(S["piece_out"], 1)

                    def exps(t):
                        for c in range(LC):
                            act.wait_ge(S["sb_ready"], n * 80 + LC * t + c + 1)
                            o = act.activation(sp[t % 4][:, c, :], sp[t % 4][:, c, :], ACT.Exp, scale=-1.0,
                                               bias=mn[t % 4][:, c:c + 1], accum_out=den[t % 4][:, c:c + 1])
                        o.then_inc(S["exp_done"], 1)

                    def pt_out(t):
                        act.wait_ge(S["ptrans"], n * 48 + 3 * t + 2)
                        if t >= 2:
                            act.wait_ge(S["av"], n * NT + t - 1)
                        act.activation(pt[t % 2][0:HL, 0:2].rearrange("p c f i -> p (c f i)"),
                                       ps[0:HL, psT[0], :], ACT.Copy).then_inc(S["pt_a"], 1)

                    def o_out(t):
                        p, v, hg = t // 4, t // 2 % 2, t % 2
                        w0 = 2 * WS * p + WS * v
                        act.wait_ge(S["av"], n * NT + t + 1)
                        act.activation(ostrip[:, hg, :, w0:w0 + WS],
                                       psO[:, 0:L].rearrange("p (h w) -> p h w", w=WS), ACT.Identity,
                                       bias=qb[:, 4 + hg:5 + hg]).then_inc(S["o_out"], 1)

                    if first:
                        for i in range(4):
                            piece_out(i)
                        exps(0)
                        for i in range(4, 8):
                            piece_out(i)
                        exps(1)
                        for i in range(8, 10):
                            piece_out(i)
                        return
                    for t in range(NT):
                        if t >= 2:
                            o_out(t - 2)
                        if not (last and t + 2 >= NT):
                            exps(t + 2)
                        made = pieces_at(t, last)
                        for i in made[:-1]:
                            piece_out(i)
                        pt_out(t)
                        for i in made[-1:]:
                            piece_out(i)
                    o_out(NT - 2)
                    o_out(NT - 1)

                strip(0, False, first=True)
                each_strip(act, strip)
                act.wait_ge(S["o_out"], b * (NS * NT) + NS * NT)
                act.activation(tick[:, 1:2], tick[:, 3:4], ACT.Copy).then_inc(S["image_done"], 1)
                act.wait_ge(S["image_done"], b * 4 + 4)

                def b1_out(q, par):
                    act.wait_ge(S["f1"], b * NCH + q + 1)
                    act.activation(b1[par][0:96], ps[0:96, par, 0:388].rearrange("p (c l) -> p c l", l=97),
                                   ACT.Copy).then_inc(S["b1_ready"], 1)

                def gate(q, par):
                    act.wait_ge(S["tg_ready"], b * NCH + q + 1)
                    act.activation(tg[par][0:96], tg[par][0:96], ACT.Sigmoid, scale=5.0).then_inc(S["gate_ready"], 1)

                def h_out(q, par):
                    act.wait_ge(S["i1"], b * NCH + q + 1)
                    act.activation(A[:, bass.ds(q * 4, 4), :],
                                   ps[0:96, 4 + par, 0:384].rearrange("p (c h) -> p c h", h=96),
                                   ACT.Copy).then_inc(S["h_ready"], 1)

                b1_out(0, 0)
                b1_out(1, 1)
                b1_out(2, 0)
                gate(0, 0)
                with act.Fori(0, NCH // 2 - 2) as i:
                    for par in (1, 0):
                        q = i * 2 + (1 if par else 2)
                        b1_out(q + 2, par)
                        gate(q, par)
                        h_out(q - 1, 1 - par)
                for q in range(NCH - 3, NCH):
                    if q + 2 < NCH:
                        b1_out(q + 2, q % 2)
                    gate(q, q % 2)
                    h_out(q - 1, 1 - q % 2)
                h_out(NCH - 1, (NCH - 1) % 2)

                def y_out(g_, par, free):
                    act.wait_ge(S["yps"], b * NG + g_ + 1)
                    if free:
                        act.wait_ge(S[f"y_out{par}"], b * (NG * 8) + (g_ - par) * 8)
                    act.activation(ys[par], ps[:, 4 + 2 * par:6 + 2 * par, 0:384], ACT.Copy).then_inc(S["y_ready"], 1)

                for par in range(2):
                    y_out(par, par, False)
                with act.Fori(1, NG // 2) as i:
                    for par in range(2):
                        y_out(i * 2 + par, par, True)
                for par in range(2):
                    act.wait_ge(S[f"y_out{par}"], b * (NG * 8) + NG * 8)
                act.wait_ge(S["agg_step"], b * 7 + 7)

            act.wait_ge(S["bnf_sqrt_in"], 1)
            act.activation(bn2s[:, 3, :], bn2s[:, 2, :], ACT.Sqrt).then_inc(S["bnf_sqrt"], 1)
            act.wait_ge(S["bnf_ready"], 1)
            with act.Fori(0, B) as b:
                for k in range(8):
                    act.wait_ge(f_in[k], b * 16 + 16)
                    act.activation(fb[k], fb[k], ACT.Gelu, scale=bn2s[:, 4, k // 4:k // 4 + 1],
                                   bias=bn2s[:, 5, k // 4:k // 4 + 1]).then_inc(f_gelu[k], 1)

        @block.vector
        def _(v):
            v.wait_ge(S["consts_in"], 16 * NCONST)
            v.tensor_scalar(nqb[:], qb[:, 0:CT], -SCALE, None, ALU.mult).then_inc(S["setup_vec"], 1)
            v.wait_ge(S["setup_pool"], 5)

            with v.Fori(0, B) as b:
                for ct in range(CT):
                    u = b * CT + ct
                    base = u * 8
                    for kk in range(24):
                        v.wait_ge(S["n_f"], u * 24 + kk + 1)
                        v.tensor_reduce(mm[:, 0, kk:kk + 1], NF[:, 4 * kk:4 * kk + 4, :], AX.XY, ALU.max)
                        last = v.tensor_reduce(mm[:, 1, kk:kk + 1], NF[:, 4 * kk:4 * kk + 4, :], AX.XY, ALU.min)
                    last.then_inc(S["n_chain"], 1)
                    v.wait_ge(S["n_chain"], base + 1)
                    v.tensor_reduce(mx[:, 0:1], mm[:, 0, :], AX.X, ALU.max).then_inc(S["n_chain"], 1)
                    v.tensor_reduce(mx[:, 1:2], mm[:, 1, :], AX.X, ALU.min).then_inc(S["n_chain"], 1)
                    v.wait_ge(S["n_chain"], base + 2)
                    v.tensor_scalar(mx[:, 2:3], mx[:, 0:1], 1e-6, None, ALU.add).then_inc(S["n_chain"], 1)
                    v.wait_ge(S["n_chain"], base + 4)
                    v.reciprocal(mx[:, 2:3], mx[:, 2:3]).then_inc(S["n_chain"], 1)
                    v.wait_ge(S["n_chain"], base + 5)
                    v.tensor_copy(rrep, mx[:, 2:3].broadcast_to([128, 32])).then_inc(S["n_r"], 1)
                    v.wait_ge(S["n_e"], u + 1)
                    v.tensor_copy(mx[:, 3:4], ps[:, 7, 511:512]).then_inc(S["n_chain"], 1)
                    v.wait_ge(S["n_chain"], base + 6)
                    v.tensor_scalar(erows[:], ps[:, 3:8, :].rearrange("p n k -> p (n k)")[:, 0:2304], mx[:, 3:4], None,
                                    ALU.subtract).then_inc(S["n_erow"], 1)
                    v.wait_ge(S["n_emt"], u * 64 + 64)
                    v.wait_ge(S["n_erow"], u + 1)
                    v.tensor_copy(tick[:, 2:3], tick[:, 3:4]).then_inc(S["n_free"], 1)
                    eb = esum[:, bass.ds(b, 1), :].rearrange("p b l -> p (b l)")
                    if ct == 0:
                        v.tensor_copy(eb, emt).then_inc(S["n_chain"], 1)
                    else:
                        v.wait_ge(S["n_chain"], base - 1)
                        v.tensor_tensor(eb, eb, emt, ALU.add).then_inc(S["n_chain"], 1)
                    v.wait_ge(S["n_chain"], base + 7)
                    v.tensor_copy(mx[:, 0:1], mx[:, 2:3]).then_inc(S["n_chain"], 1)
                    v.wait_ge(S["n_chain"], base + 8)
            v.wait_ge(S["taps_in"], 16 * NTAPS)
            m = [0]

            def link(ins):
                m[0] += 1
                ins.then_inc(S["m_chain"], 1)
                v.wait_ge(S["m_chain"], m[0])

            v.tensor_scalar(esum[:], esum[:], 1.0 / C, None, ALU.mult).then_inc(S["n_ec"], 1)
            v.wait_ge(S["n_et"], 1)
            for b in range(B):
                last = v.tensor_copy(emap[:, b, 1:97], ps[0:96, 4 + b // 4, 96 * (b % 4):96 * (b % 4) + 96])
            link(last)
            for d in range(3):
                link(v.tensor_scalar(band[0:96, d], shift[0:96, 0], taps[0:96, 3 * d:3 * d + 1], None, ALU.mult))
                for e in (1, 2):
                    link(v.scalar_tensor_tensor(band[0:96, d], shift[0:96, e], taps[0:96, 3 * d + e:3 * d + e + 1],
                                                band[0:96, d], ALU.mult, ALU.add))
            v.tensor_scalar(sc[0:96, 16:17], sc[0:96, 2:3], 1.0 / W, None, ALU.mult).then_inc(S["m_band"], 1)
            v.wait_ge(S["m_cmap"], B)
            for b in range(B):
                last = v.bn_stats(st6[0:96, b], cmap[0:96, b])
            link(last)
            link(v.bn_aggr(sc[0:96, 5:7], st6[0:96].rearrange("p b s -> p (b s)")))
            v.tensor_copy(sc[0:96, 7:8], sc[0:96, 5:6]).then_inc(S["m_mean_in"], 1)
            v.wait_ge(S["m_mean"], 1)
            link(v.tensor_copy(sc[0:96, 8:9], ps[0:96, 2, 0:1]))
            link(v.tensor_tensor(sc[0:96, 9:10], sc[0:96, 5:6], sc[0:96, 8:9], ALU.subtract))
            link(v.tensor_tensor(sc[0:96, 9:10], sc[0:96, 9:10], sc[0:96, 9:10], ALU.mult))
            v.tensor_tensor(sc[0:96, 10:11], sc[0:96, 9:10], sc[0:96, 6:7], ALU.add).then_inc(S["m_var_in"], 1)
            v.wait_ge(S["m_var"], 1)
            link(v.tensor_scalar(sc[0:96, 11:12], ps[0:96, 3, 0:1], 1e-5, None, ALU.add))
            v.reciprocal(sc[0:96, 11:12], sc[0:96, 11:12]).then_inc(S["m_sqrt_in"], 1)
            v.wait_ge(S["m_sqrt"], 1)
            link(v.tensor_tensor(sc[0:96, 13:14], sc[0:96, 12:13], sc[0:96, 0:1], ALU.mult))
            link(v.tensor_tensor(sc[0:96, 15:16], sc[0:96, 8:9], sc[0:96, 13:14], ALU.mult))
            v.tensor_tensor(sc[0:96, 14:15], sc[0:96, 1:2], sc[0:96, 15:16], ALU.subtract).then_inc(S["m_ab"], 1)
            v.wait_ge(S["m_ng"], 1)
            link(v.tensor_scalar(ngb[0:96], ngb[0:96], sc[0:96, 4:5], None, ALU.mult))
            v.wait_ge(S["m_sig"], 1)
            v.tensor_tensor(mask[:], le[0:96], ngb[0:96].unsqueeze(2).broadcast_to([96, B, 96]),
                            ALU.mult).then_inc(S["m_done"], 1)
            v.wait_ge(S["bias_in"], 16 * NBIAS)
            v.tensor_scalar(negbias[:], negbias[:], -1.0, None, ALU.mult).then_inc(S["setup_vec"], 1)
            v.wait_ge(S["setup_vec"], 2)
            v.wait_ge(S["m_done"], 1)

            with v.Fori(0, B) as b:
                def strip(s, par, last, first=False):
                    n = b * NS + s

                    def scores_out(t):
                        waits = [(S["scores"], n * NT + t + 1)]
                        if t >= 4:
                            waits.append((S["ptrans"], n * 48 + 3 * (t - 3)))
                        wait_apart(v, *waits)
                        for c in range(LC):
                            v.tensor_tensor_reduce(
                                out=sp[t % 4][:, c, :], in0=psS[t % 2][:, c // 3, L * (c % 3):L * (c % 3) + L],
                                in1=negbias[:, t % 2, c, :], scale=1.0, scalar=BIG, op0=ALU.add, op1=ALU.min,
                                accum_out=mn[t % 4][:, c:c + 1]).then_inc(S["sb_ready"], 1)

                    def recip(t):
                        v.wait_ge(S["exp_done"], n * NT + t + 1)
                        v.reciprocal(rden[t % 4], den[t % 4]).then_inc(S["rden_ready"], 1)

                    def pt_out(t):
                        for un in (2, 1):
                            v.wait_ge(S["ptrans"], n * 48 + 3 * t + (1 if un == 2 else 3))
                            if un == 2 and t >= 2:
                                v.wait_ge(S["av"], n * NT + t - 1)
                            w = 512 if un == 1 else 256
                            v.tensor_copy(pt[t % 2][0:HL, 2 * un:2 * un + w // 256].rearrange("p c f i -> p (c f i)"),
                                          ps[0:HL, psT[un], 0:w]).then_inc(S["pt_d"], 1)

                    taps_order = [4, 0, 1, 2, 3, 5, 6, 7, 8]

                    def lpe_step(k):
                        ct, tap = k % 2, taps_order[k // 2]
                        dy, dx = tap // 3, tap % 3
                        if k == 0:
                            v.wait_ge(S[f"xs_in{par}"], (n - par) * 24 + 48)
                        if tap == 4:
                            v.tensor_scalar(lpe[:, ct], xs[par][:, ct, 1:WS + 1, :], lw[:, ct, 4:5], lb[:, ct:ct + 1],
                                            ALU.mult, ALU.add).then_inc(S["lpe_step"], 1)
                            return
                        v.wait_ge(S["lpe_step"], n * 18 + k - 1)
                        w0, w1 = max(0, 1 - dx), min(W, W + 1 - dx)
                        v.scalar_tensor_tensor(lpe[:, ct, :, w0:w1], xs[par][:, ct, dy:dy + WS, w0 + dx - 1:w1 + dx - 1],
                                               lw[:, ct, tap:tap + 1], lpe[:, ct, :, w0:w1],
                                               ALU.mult, ALU.add).then_inc(S["lpe_step"], 1)

                    if first:
                        for t in range(3):
                            scores_out(t)
                        recip(0)
                        recip(1)
                        return
                    v.tensor_copy(mrow[0:96], mask[:, bass.ds(b, 1), bass.ds(s * WS, WS)]
                                  .rearrange("p b h -> p (b h)")).then_inc(S["mrow_ready"], 1)
                    for t in range(NT):
                        if not (last and t + 3 >= NT):
                            scores_out(t + 3)
                        if not (last and t + 2 >= NT):
                            recip(t + 2)
                        pt_out(t)
                        for k in range(18 * t // (NT - 1), 18 * (t + 1) // (NT - 1)):
                            if k < 18:
                                lpe_step(k)
                    v.wait_ge(S["mrow_ready"], n + 1)
                    for r in range(WS):
                        v.wait_ge(S["row_ps"], n * WS + r + 1)
                        rp = ps[0:96, r % 4, :]
                        v.scalar_tensor_tensor(rowt[r % 2][0:96], rp[:, C:2 * C], mrow[0:96, r:r + 1], pb[:],
                                               ALU.mult, ALU.add).then_inc(S["row_mask"], 1)
                        v.wait_ge(S["row_mask"], n * WS + r + 1)
                        v.tensor_tensor(A[:, :, bass.ds(s * WS + r, 1)].rearrange("p c h -> p (c h)"), rp[:, 0:C],
                                        rowt[r % 2][0:96], ALU.add).then_inc(S["a_row"], 1)
                    v.wait_ge(S["a_row"], n * WS + WS)

                strip(0, 0, False, first=True)
                each_strip_by_parity(v, strip)
                v.tensor_copy(tick[:, 2:3], tick[:, 3:4]).then_inc(S["image_done"], 1)
                v.wait_ge(S["image_done"], b * 4 + 4)

                def centre(q, par):
                    v.wait_ge(S["f2"], b * NCH + q + 1)
                    v.tensor_copy(msb[par][0:96], ps[0:96, 2 + par, 384:388])
                    v.tensor_scalar(tg[par][0:96].rearrange("p c l -> p (c l)").bitcast(U32),
                                    ps[0:96, 2 + par, 0:384].bitcast(U32), 0x7FFFFFFF, None,
                                    ALU.bitwise_and).then_inc(S["abs_ready"], 1)

                def gated(q, par):
                    v.wait_ge(S["gate_ready"], b * NCH + q + 1)
                    v.tensor_tensor(gs[par][0:96], ps[0:96, 2 + par, 0:384].rearrange("p (c l) -> p c l", l=96),
                                    tg[par][0:96], ALU.mult).then_inc(S["g_ready"], 1)

                centre(0, 0)
                with v.Fori(0, NCH // 2 - 1) as i:
                    for par in range(2):
                        q = i * 2 + par
                        centre(q + 1, 1 - par)
                        gated(q, par)
                centre(NCH - 1, 1)
                gated(NCH - 2, 0)
                gated(NCH - 1, 1)

                def z_out(g_, par):
                    v.wait_ge(S[f"xc_in{par}"], b * (NG * 8) + (g_ - par) * 8 + 16)
                    v.wait_ge(S["zps"], b * NG + g_ + 1)
                    v.tensor_tensor(zs[par], ps[:, 2 * par:2 * par + 2, 0:384], xc[par], ALU.add).then_inc(S["z_ready"], 1)

                def y_stats(g_, par):
                    v.wait_ge(S["y_ready"], b * NG + g_ + 1)
                    for ct in range(CT):
                        last = v.bn_stats(stats[:, ct, bass.ds(g_, 1), :].rearrange("p g s -> p (g s)"), ys[par][:, ct, :])
                    last.then_inc(S["stat"], 1)

                z_out(0, 0)
                with v.Fori(0, NG // 2 - 1) as i:
                    for par in range(2):
                        z_out(i * 2 + par + 1, 1 - par)
                        y_stats(i * 2 + par, par)
                z_out(NG - 1, 1)
                y_stats(NG - 2, 0)
                y_stats(NG - 1, 1)
                wait_apart(v, (S["stat"], b * NG + NG))
                base = b * 7
                for ct in range(CT):
                    v.bn_aggr(ag[:, ct, :], stats[:, ct].rearrange("p g s -> p (g s)")).then_inc(S["agg_step"], 1)
                v.wait_ge(S["agg_step"], base + 2)
                for ct in range(CT):
                    dst = agg[:, ct, bass.ds(b, 1), :].rearrange("p b s -> p (b s)")
                    v.tensor_copy(dst[:, 1:2], ag[:, ct, 0:1]).then_inc(S["agg_step"], 1)
                    v.tensor_scalar(dst[:, 2:3], ag[:, ct, 1:2], float(HW), None, ALU.mult).then_inc(S["agg_step"], 1)
                v.wait_ge(S["agg_step"], base + 6)
                v.tensor_copy(ag[:, 0, 0:1], ag[:, 0, 1:2]).then_inc(S["agg_step"], 1)
                for par in range(2):
                    v.wait_ge(S[f"y_out{par}"], b * (NG * 8) + NG * 8)
                v.wait_ge(S["agg_step"], base + 7)

            f = [0]

            def flink(ins):
                f[0] += 1
                ins.then_inc(S["bnf_step"], 1)
                v.wait_ge(S["bnf_step"], f[0])

            flink(v.memset(agg[:, :, :, 0:1], float(HW)))
            for ct in range(CT):
                flink(v.bn_aggr(bn2s[:, 0:2, ct], agg[:, ct].rearrange("p b s -> p (b s)")))
            flink(v.tensor_scalar(bn2s[:, 2, :], bn2s[:, 1, :], 1e-5, None, ALU.add))
            v.reciprocal(bn2s[:, 2, :], bn2s[:, 2, :]).then_inc(S["bnf_sqrt_in"], 1)
            v.wait_ge(S["bnf_sqrt"], 1)
            flink(v.tensor_tensor(bn2s[:, 4, :], bn2s[:, 3, :], bn2[:, 0, :], ALU.mult))
            flink(v.tensor_tensor(bn2s[:, 1, :], bn2s[:, 0, :], bn2s[:, 4, :], ALU.mult))
            v.tensor_tensor(bn2s[:, 5, :], bn2[:, 1, :], bn2s[:, 1, :], ALU.subtract).then_inc(S["bnf_ready"], 1)

        @block.tensor
        def _(pe):
            def mmul(o, l, r, start=True, stop=True):
                return nc.tensor.matmul(o, l, r, start=start, stop=stop)

            pe.wait_ge(S["consts_in"], 16 * NCONST)
            pe.wait_ge(S["setup_pool"], 5)
            with pe.Fori(0, B * CT) as u:
                for q in range(32):
                    g = q // 4
                    if q % 4 == 0:
                        pe.wait_ge(n_x[g], u * 16 + 16)
                    if q >= 3:
                        pe.wait_ge(S["n_b1"], u * 32 + q - 2)
                    for i in range(4):
                        last = mmul(ps[0:96, q % 3, 96 * i:96 * i + 96], xg[g][0:96, 4 * (q % 4) + i, :],
                                    dct[:, 0:96])
                    last.then_inc(S["n_st1"], 1)
                pe.wait_ge(S["n_b1"], u * 32 + 32)
                pe.wait_ge(S["n_free"], u + 1)
                for kk in range(24):
                    if kk >= 4:
                        pe.wait_ge(S["n_f"], u * 24 + kk - 3)
                    for i in range(4):
                        last = mmul(ps[:, 3 + kk % 4, 96 * i:96 * i + 96], NB1[:, :, 4 * kk + i], dct[:, 0:96])
                    last.then_inc(S["n_st2"], 1)
                pe.wait_ge(S["n_f"], u * 24 + 24)
                pe.wait_ge(S["n_r"], u + 1)
                flat = NF.rearrange("p k l -> p (k l)")
                for n in range(5):
                    w = min(512, 2304 - 512 * n)
                    for j in range(4):
                        mmul(ps[32 * j:32 * j + 32, 3 + n, 0:w], rrep, flat[:, 2304 * j + 512 * n:2304 * j + 512 * n + w])
                for j in range(4):
                    last = mmul(ps[32 * j:32 * j + 32, 7, 511:512], rrep, mx[:, 1:2])
                last.then_inc(S["n_e"], 1)
            pe.wait_ge(S["n_ec"], 1)
            for b in range(B):
                last = nc.tensor.transpose(ps[0:96, 4 + b // 4, 96 * (b % 4):96 * (b % 4) + 96], esum[:, b, :],
                                           eye[0:96, 0:96])
            last.then_inc(S["n_et"], 1)
            pe.wait_ge(S["m_band"], 1)
            for g in range(0, B, 4):
                nb = min(4, B - g)
                for d in range(3):
                    last = mmul(ps[0:96, g // 4, 0:96 * nb], band[0:96, d], emap[:, g:g + nb, d:d + 96],
                                start=d == 0, stop=d == 2)
            last.then_inc(S["m_conv"], 1)
            pe.wait_ge(S["m_mean_in"], 1)
            mmul(ps[0:96, 2, 0:1], ones96[0:96], sc[0:96, 7:8]).then_inc(S["m_mean"], 1)
            pe.wait_ge(S["m_var_in"], 1)
            mmul(ps[0:96, 3, 0:1], ones96[0:96], sc[0:96, 10:11]).then_inc(S["m_var"], 1)
            pe.wait_ge(S["m_le"], B)
            mmul(ps[0:96, 4, 0:B], ones96[0:96], accb[0:96]).then_inc(S["m_pool"], 1)
            pe.wait_ge(S["m_done"], 1)
            pe.wait_ge(S["setup_vec"], 2)

            with pe.Fori(0, B) as b:
                def strip(s, last, first=False):
                    n = b * NS + s

                    def piece(i):
                        p, k = i // NPC, i % NPC
                        if k == 0:
                            pe.wait_ge(S["xw_ready"], n * NP + p + 1)
                        if i:
                            pe.wait_ge(S["piece_out"], n * (NP * NPC) + i)
                        xp = xw[p % 2]
                        if k < 6:
                            for kt in range(CT):
                                last = mmul(ps[:, psM, 0:2 * L], wqkv[:, kt, 128 * k:128 * k + 128], xp[:, kt, :],
                                            start=kt == 0, stop=kt == CT - 1)
                        else:
                            for f in range(2):
                                t0 = L * (k - 6) + HL * f
                                for ct in range(CT):
                                    at = C * f + 128 * ct
                                    last = nc.tensor.transpose(ps[0:HL, psM, at:at + 128], vt[:, ct, t0:t0 + HL], eye[:])
                        last.then_inc(S["piece"], 1)

                    def score(t):
                        p, v, hg = t // 4, t // 2 % 2, t % 2
                        pe.wait_ge(S["qbd_ready"], n * NT + t + 1)
                        pe.wait_ge(S["piece_out"], (n * NP + p) * NPC + 3 + hg)
                        if t >= 2:
                            pe.wait_ge(S["sb_ready"], n * 80 + LC * (t - 1))
                        for c in range(LC):
                            last = mmul(psS[t % 2][:, c // 3, L * (c % 3):L * (c % 3) + L],
                                        qbd[t % 2][:, c].rearrange("p j i -> p (j i)"),
                                        k_sb[p % 2][:, hg, L * v:L * v + L])
                        last.then_inc(S["scores"], 1)

                    def transposes(t):
                        pe.wait_ge(S["norm_done"], n * NT + t + 1)
                        for un in (2, 0, 1):
                            if t >= 1:
                                if un == 0:
                                    pe.wait_ge(S["pt_a"], n * NT + t)
                                else:
                                    pe.wait_ge(S["pt_d"], n * 2 * NT + 2 * (t - 1) + 3 - un)
                            if t >= 2 and un == 2:
                                pe.wait_ge(S["o_out"], n * NT + t - 1)
                            for c in range(2 * un, min(2 * un + 2, LC)):
                                for f in range(2):
                                    at = ((c % 2) * 2 + f) * 128
                                    last = nc.tensor.transpose(ps[0:HL, psT[un], at:at + 128],
                                                               sp[t % 4][:, c, HL * f:HL * f + HL], eye[:])
                            last.then_inc(S["ptrans"], 1)

                    def attend(t):
                        p, v, hg = t // 4, t // 2 % 2, t % 2
                        pe.wait_ge(S["pt_a"], n * NT + t + 1)
                        pe.wait_ge(S["pt_d"], n * 2 * NT + min(2 * t + 3, 2 * NT))
                        pe.wait_ge(S["piece_out"], (n * NP + p) * NPC + 7 + v)
                        if t >= 1:
                            pe.wait_ge(S["o_out"], n * NT + t)
                        for f in range(2):
                            for j in range(HG):
                                ch = 128 * hg + 32 * j
                                last = mmul(psO[32 * j:32 * j + 32, :],
                                            v_sb[p % 2][0:HL, v, f, ch:ch + 32],
                                            pt[t % 2][0:HL, :, f, 32 * j:32 * j + 32], start=f == 0, stop=f == 1)
                        last.then_inc(S["av"], 1)

                    if first:
                        for i in range(4):
                            piece(i)
                        for t in range(3):
                            score(t)
                        for i in range(4, 10):
                            piece(i)
                        return
                    for t in range(NT):
                        if not (last and t + 3 >= NT):
                            score(t + 3)
                        made = pieces_at(t, last)
                        for i in made[:-1]:
                            piece(i)
                        transposes(t)
                        for i in made[-1:]:
                            piece(i)
                        if t >= 1:
                            attend(t - 1)
                    attend(NT - 1)
                    if not last:
                        pe.wait_ge(S["sb_ready"], n * 80 + LC * (NT + 3))
                    pe.wait_ge(S["o_out"], n * NT + NT)
                    pe.wait_ge(S["lpe_step"], n * 18 + 18)
                    for r in range(WS):
                        if r >= 4:
                            pe.wait_ge(S["a_row"], n * WS + r - 3)
                        for ct in range(CT):
                            nc.tensor.transpose(ps[0:96, r % 4, C + 128 * ct:C + 128 * ct + 128], lpe[:, ct, r, :], eye[:])
                        for ct in range(CT):
                            last = mmul(ps[0:96, r % 4, 0:C], ostrip[:, ct, r, :], wproj[:, ct, :],
                                        start=ct == 0, stop=ct == CT - 1)
                        last.then_inc(S["row_ps"], 1)
                    pe.wait_ge(S["a_row"], n * WS + WS)

                strip(0, False, first=True)
                each_strip(pe, strip)
                mmul(ps[0:96, psM, 0:1], eye[:, 0:96], eye[:, 0:1]).then_inc(S["image_done"], 1)
                pe.wait_ge(S["image_done"], b * 4 + 4)

                def f1(q):
                    if q >= 2:
                        pe.wait_ge(S["b1_ready"], b * NCH + q - 1)
                    for i in range(4):
                        last = mmul(ps[0:96, q % 2, 97 * i:97 * i + 97], A[:, 4 * q + i, :], dct[:])
                    last.then_inc(S["f1"], 1)

                def f2(q):
                    pe.wait_ge(S["b1_ready"], b * NCH + q + 1)
                    if q >= 2:
                        pe.wait_ge(S["g_ready"], b * NCH + q - 1)
                    mmul(ps[0:96, 2 + q % 2, 0:384], dct[:, 0:96], b1[q % 2][0:96, :, 0:96])
                    mmul(ps[0:96, 2 + q % 2, 384:388], meanm[:], b1[q % 2][0:96, :, 96]).then_inc(S["f2"], 1)

                def i1(q):
                    pe.wait_ge(S["g_ready"], b * NCH + q + 1)
                    if q >= 2:
                        pe.wait_ge(S["h_ready"], b * NCH + q - 1)
                    for i in range(4):
                        last = mmul(ps[0:96, 4 + q % 2, 96 * i:96 * i + 96], gs[q % 2][0:96, i, :], inv[:])
                    last.then_inc(S["i1"], 1)

                f1(0)
                f1(1)
                f2(0)
                for q in range(NCH):
                    if q + 2 < NCH:
                        f1(q + 2)
                    if q + 1 < NCH:
                        f2(q + 1)
                    if q >= 1:
                        i1(q - 1)
                i1(NCH - 1)
                pe.wait_ge(S["h_ready"], b * NCH + NCH)

                def zrows(g):
                    if g >= 2:
                        pe.wait_ge(S["z_ready"], b * NG + g - 1)
                    for ct in range(CT):
                        for i in range(4):
                            last = mmul(ps[:, 2 * (g % 2) + ct, 96 * i:96 * i + 96],
                                        A[:, 128 * ct:128 * ct + 128, 4 * g + i], inv[:])
                    last.then_inc(S["zps"], 1)

                def yrows(g):
                    pe.wait_ge(S["z_ready"], b * NG + g + 1)
                    if g >= 2:
                        pe.wait_ge(S["y_ready"], b * NG + g - 1)
                    for mt in range(CT):
                        for kt in range(CT):
                            last = mmul(ps[:, 4 + 2 * (g % 2) + mt, 0:384], wfr[:, kt, 128 * mt:128 * mt + 128],
                                        zs[g % 2][:, kt, :], start=kt == 0, stop=kt == CT - 1)
                    last.then_inc(S["yps"], 1)

                pe.wait_ge(S["wfr_in"], b * 16 + 16)
                zrows(0)
                for g in range(NG):
                    if g + 1 < NG:
                        zrows(g + 1)
                    yrows(g)
                for par in range(2):
                    pe.wait_ge(S[f"y_out{par}"], b * (NG * 8) + NG * 8)
                pe.wait_ge(S["agg_step"], b * 7 + 7)


_NAMES = ("x", "wqkvT", "wprojT", "wfrT", "qkv_b", "proj_b", "lpe_w", "lpe_b", "lpe_scale", "rpb_rev", "ec_w",
          "bn1_g", "bn1_b", "nl_w", "nl_b", "bn2_g", "bn2_b")


def lay_out(inputs):
    p = "L0_conv_"
    g = {k.removeprefix(p): np.asarray(v) for k, v in inputs.items()}
    t = g["rpb_table"].T.reshape(HEADS, 2 * WS - 1, 2 * WS - 1)
    arrays = {
        "x": g["x"], "wqkvT": g["qkv_w"].T, "wprojT": g["proj_w"].T, "wfrT": g["fr_w"].reshape(C, C).T,
        "qkv_b": g["qkv_b"].reshape(-1, 128).T, "proj_b": g["proj_b"],
        "lpe_w": g["lpe_w"].reshape(C, 9), "lpe_b": g["lpe_b"].reshape(-1, 128).T,
        "lpe_scale": g["lpe_scale"], "rpb_rev": t[:, ::-1, ::-1], "ec_w": g["ec_w"].reshape(9),
        "bn1_g": g["bn1_g"], "bn1_b": g["bn1_b"], "nl_w": g["nl_w"].reshape(1), "nl_b": g["nl_b"],
        "bn2_g": g["bn2_g"].reshape(-1, 128).T, "bn2_b": g["bn2_b"].reshape(-1, 128).T,
    }
    arrays.update(shape_constants())
    return {k: np.ascontiguousarray(v) for k, v in arrays.items()}


def kernel(**inputs):
    import concourse.bacc as _bacc
    from concourse.bass_utils import run_bass_kernel_spmd as _run

    arrays = lay_out(inputs)
    B = arrays["x"].shape[0]
    nc = _bacc.Bacc("TRN2", target_bir_lowering=False, num_devices=1)
    aps = {k: nc.dram_tensor(f"in_{k}", v.shape, mybir.dt.from_np(v.dtype), kind="ExternalInput").ap()
           for k, v in arrays.items()}
    out = nc.dram_tensor("out_0", (B, C, HW), F32, kind="ExternalOutput").ap()
    build(nc, aps, out, B)
    r = _run(nc, [{f"in_{k}": v for k, v in arrays.items()}], core_ids=[0])
    return r.results[0]["out_0"].reshape(B, C, H, W)
```
